# Optimizing a Trainium2 kernel written in Bass

```python
import numpy as np
import jax
import jax.numpy as jnp

def _softmax(x, axis=-1):
    return jax.nn.softmax(x, axis=axis)

def _gelu(x):
    return jax.nn.gelu(x, approximate=True)

def _silu(x):
    return jax.nn.silu(x)

def _sigmoid(x):
    return jax.nn.sigmoid(x)

def _layernorm(x, axis=-1, eps=1e-05):
    m = jnp.mean(x, axis=axis, keepdims=True)
    v = jnp.var(x, axis=axis, keepdims=True)
    return (x - m) / jnp.sqrt(v + eps)

def _scatter_add(tgt, idx, src, axis=0):
    return tgt.at[idx].add(src)

def _segment_sum(src, seg, n):
    return jax.ops.segment_sum(src, seg, n)
kernel_name = 'mk_gnn_resnorm_d2_gnn_r8_04b5eb'

def setup_inputs(seed: int=0):
    np.random.seed(seed)
    _w = jnp.asarray

    def _rec_inputs():
        import jax
        import jax.numpy as jnp
        _gk = jax.random.key(seed)
        x = -0.0009044 + 1 * jax.random.normal(jax.random.fold_in(_gk, 1), (12500, 16), jnp.float32)
        _s = jax.random.randint(jax.random.fold_in(_gk, 2), (200000,), 0, 12500, jnp.int32)
        _d = jax.random.randint(jax.random.fold_in(_gk, 3), (200000,), 0, 12500, jnp.int32)
        _loop = jnp.arange(12500, dtype=jnp.int32)
        src = jnp.concatenate([_s, _d, _loop])
        dst = jnp.concatenate([_d, _s, _loop])
        _o = jnp.argsort(dst, stable=True)
        src = src[_o]
        dst = dst[_o]
        return (x, src, dst)
    x, src, dst = _rec_inputs()

    def _L0_gnn_setup():
        import jax, jax.numpy as jnp
        import numpy as np
        N_NODES = 12500
        N_EDGES = 200000

        def _sage_conv(x, edge_index, W_l, b, W_r, num_nodes):
            src, dst = (edge_index[0], edge_index[1])
            msg_sum = jax.ops.segment_sum(x[src], dst, num_segments=num_nodes)
            deg = jax.ops.segment_sum(jnp.ones((edge_index.shape[1],), x.dtype), dst, num_segments=num_nodes)
            agg = msg_sum / jnp.maximum(deg, 1.0)[:, None]
            return agg @ W_l + b + x @ W_r
        key = jax.random.key(seed)
        ks = jax.random.split(key, 8)
        x = jax.random.normal(ks[0], (N_NODES, 16), dtype=jnp.float32)
        edge_index = jax.random.randint(ks[1], (2, N_EDGES), 0, N_NODES, dtype=jnp.int64)
        s1 = 1.0 / np.sqrt(16.0)
        s2 = 1.0 / np.sqrt(32.0)
        W1_l = jax.random.normal(ks[2], (16, 32), dtype=jnp.float32) * s1
        b1 = jax.random.normal(ks[3], (32,), dtype=jnp.float32) * s1
        W1_r = jax.random.normal(ks[4], (16, 32), dtype=jnp.float32) * s1
        W2_l = jax.random.normal(ks[5], (32, 16), dtype=jnp.float32) * s2
        b2 = jax.random.normal(ks[6], (16,), dtype=jnp.float32) * s2
        W2_r = jax.random.normal(ks[7], (32, 16), dtype=jnp.float32) * s2
        return {'x': x, 'edge_index': edge_index, 'W1_l': W1_l, 'b1': b1, 'W1_r': W1_r, 'W2_l': W2_l, 'b2': b2, 'W2_r': W2_r}
    _L0_gnn_all = _L0_gnn_setup()
    _L0_gnn_in = {k: v for k, v in _L0_gnn_all.items() if k in ('W1_l', 'b1', 'W1_r', 'W2_l', 'b2', 'W2_r')}
    del _L0_gnn_all

    def _L1_gnn_setup():
        import jax, jax.numpy as jnp
        import numpy as np
        STALK_DIM = 16
        N_NODES = 6250
        N_EDGES = 50000
        HIDDEN = 64
        key = jax.random.key(seed)
        k1, k2, k3, k4 = jax.random.split(key, 4)
        d = STALK_DIM
        x = jax.random.normal(k1, (N_NODES, d), dtype=jnp.float32)
        edge_index = jax.random.randint(k2, (2, N_EDGES), 0, N_NODES, dtype=jnp.int64)
        W1 = jax.random.normal(k3, (HIDDEN, 2 * d), dtype=jnp.float32) * (1.0 / np.sqrt(2 * d))
        b1 = jnp.zeros((HIDDEN,), dtype=jnp.float32)
        W2 = jax.random.normal(k4, (d, HIDDEN), dtype=jnp.float32) * (1.0 / np.sqrt(HIDDEN))
        b2 = jnp.zeros((d,), dtype=jnp.float32)
        return {'x': x, 'edge_index': edge_index, 'W1': W1, 'b1': b1, 'W2': W2, 'b2': b2}
    _L1_gnn_all = _L1_gnn_setup()
    _L1_gnn_in = {k: v for k, v in _L1_gnn_all.items() if k in ('W1', 'b1', 'W2', 'b2')}
    del _L1_gnn_all
    return {'x': x, 'src': src, 'dst': dst, 'L0_gnn_W1_l': _L0_gnn_in['W1_l'], 'L0_gnn_b1': _L0_gnn_in['b1'], 'L0_gnn_W1_r': _L0_gnn_in['W1_r'], 'L0_gnn_W2_l': _L0_gnn_in['W2_l'], 'L0_gnn_b2': _L0_gnn_in['b2'], 'L0_gnn_W2_r': _L0_gnn_in['W2_r'], 'L1_gnn_W1': _L1_gnn_in['W1'], 'L1_gnn_b1': _L1_gnn_in['b1'], 'L1_gnn_W2': _L1_gnn_in['W2'], 'L1_gnn_b2': _L1_gnn_in['b2']}

def reference(x, src, dst, L0_gnn_W1_l, L0_gnn_b1, L0_gnn_W1_r, L0_gnn_W2_l, L0_gnn_b2, L0_gnn_W2_r, L1_gnn_W1, L1_gnn_b1, L1_gnn_W2, L1_gnn_b2):
    import jax
    import jax.numpy as jnp

    def _L0_gnn_ref(x, edge_index, W1_l, b1, W1_r, W2_l, b2, W2_r):
        import jax, jax.numpy as jnp
        import numpy as np
        N_NODES = 12500
        N_EDGES = 200000

        def _sage_conv(x, edge_index, W_l, b, W_r, num_nodes):
            src, dst = (edge_index[0], edge_index[1])
            msg_sum = jax.ops.segment_sum(x[src], dst, num_segments=num_nodes)
            deg = jax.ops.segment_sum(jnp.ones((edge_index.shape[1],), x.dtype), dst, num_segments=num_nodes)
            agg = msg_sum / jnp.maximum(deg, 1.0)[:, None]
            return agg @ W_l + b + x @ W_r
        n = x.shape[0]
        h = _sage_conv(x, edge_index, W1_l, b1, W1_r, n)
        h = jax.nn.relu(h)
        out = _sage_conv(h, edge_index, W2_l, b2, W2_r, n)
        return out

    def _L1_gnn_ref(x, edge_index, W1, b1, W2, b2):
        import jax, jax.numpy as jnp
        import numpy as np
        STALK_DIM = 16
        N_NODES = 6250
        N_EDGES = 50000
        HIDDEN = 64
        d = x.shape[1]
        n = x.shape[0]
        src, dst = (edge_index[0], edge_index[1])
        xs, xd = (x[src], x[dst])

        def reflection(a, b):
            h = jax.nn.relu(jnp.concatenate([a, b], axis=1) @ W1.T + b1)
            return h @ W2.T + b2

        def householder(v):
            vn = v / jnp.maximum(jnp.linalg.norm(v, axis=1, keepdims=True), 1e-12)
            return jnp.eye(d, dtype=v.dtype)[None] - 2.0 * vn[:, :, None] * vn[:, None, :]
        F_s = householder(reflection(xs, xd))
        F_d = householder(reflection(xd, xs))
        L_sd = -jnp.einsum('eki,ekj->eij', F_s, F_d)
        ones_e = jnp.ones(src.shape[0], dtype=x.dtype)
        deg = jnp.zeros(n, dtype=x.dtype).at[src].add(ones_e).at[dst].add(ones_e)
        deg_inv_sqrt = 1.0 / jnp.sqrt(jnp.maximum(deg, 1e-05))
        coef = deg_inv_sqrt[src] * deg_inv_sqrt[dst]
        msg_s = coef[:, None] * jnp.einsum('eij,ej->ei', L_sd, xd)
        msg_d = coef[:, None] * jnp.einsum('eji,ej->ei', L_sd, xs)
        out = x - jnp.zeros_like(x).at[src].add(msg_s) - jnp.zeros_like(x).at[dst].add(msg_d)
        return jax.nn.relu(out)
    edge_index = jnp.stack([src, dst])
    x = _layernorm(x + _L0_gnn_ref(x, edge_index, L0_gnn_W1_l, L0_gnn_b1, L0_gnn_W1_r, L0_gnn_W2_l, L0_gnn_b2, L0_gnn_W2_r), axis=-1)
    x = _layernorm(x + _L1_gnn_ref(x, edge_index, L1_gnn_W1, L1_gnn_b1, L1_gnn_W2, L1_gnn_b2), axis=-1)
    return x

_drawn_inputs = setup_inputs


def setup_inputs(seed=0):
    import zlib

    import numpy as np

    out = dict(_drawn_inputs(seed))
    spreads = {'L1_gnn_b1': (0.0, 0.8), 'L1_gnn_b2': (0.0, 0.658)}
    factors = {}
    for name, (base, spread) in spreads.items():
        noise = np.random.default_rng([zlib.crc32(name.encode()), seed]).standard_normal(out[name].shape)
        drawn = base * np.exp(spread * noise) if base else spread * noise
        out[name] = jnp.asarray(drawn.astype(out[name].dtype))
    for name, factor in factors.items():
        out[name] = (out[name] * factor).astype(out[name].dtype)
    return out
```

```python
import concourse.bass as bass
from concourse import mybir
from contextlib import ExitStack

fp32 = mybir.dt.float32
bf16 = mybir.dt.bfloat16
i32 = mybir.dt.int32
ALU = mybir.AluOpType
ACT = mybir.ActivationFunctionType
AX = mybir.AxisListType.X

P = 128
F = 16
NODES = 12500
EDGES = 412500
BLOCKS = -(-NODES // P)
PAD_NODE = BLOCKS * P - 1
GROUP = 4
GROUPS = -(-BLOCKS // GROUP)
NBP = GROUPS * GROUP
HID1, HID2 = 32, 64
CH = 8
PAIR = 2 * CH


def up(n, m):
    return -(-n // m) * m


NT0 = up(-(-EDGES // P), PAIR)
NT1 = up((NT0 * P + BLOCKS * (P - 1)) // P, PAIR)
NTL = NT1 + PAIR
NT2 = up((NT1 * P + BLOCKS * (P - 1)) // P, 2 * PAIR)
NTB = up(max(NTL, NT2), P)
ROW = F + 1
NO_LANE = 255
ZROW = 1088
LN_EPS = 1e-5
BANK = 512
FILLS = 8
NORM_EPS2 = 1e-24


class Chain:

    def __init__(self, eng, sem):
        self.eng, self.sem, self.n, self.base = eng, sem, 0, None

    def __call__(self, ins):
        ins.then_inc(self.sem, 1)
        self.n += 1
        self.eng.wait_ge(self.sem, self.n if self.base is None else self.base + self.n)

    def turn(self, i, per_turn):
        self.base, self.n = i * per_turn, 0


def gnn(nc, x, src, dst, W1l, b1, W1r, W2l, b2, W2r, V1, c1, V2, c2, out):
    ctx = ExitStack()
    sems = {}

    def sem(name):
        sems[name] = ctx.enter_context(nc.semaphore(name))
        return sems[name]

    def sbuf(stack, name, shape, dt=fp32):
        return stack.enter_context(nc.sbuf_tensor(name, shape, dt))

    def banks(stack, name, n=1):
        return stack.enter_context(nc.psum_tensor(name, [P, n, BANK], fp32))

    def view(bank, n, m):
        return bank[:, 0:n * m].rearrange("p (n m) -> p n m", n=n)

    x_table = nc.dram_tensor("x_table", [BLOCKS * P, F], fp32).ap()
    h_table = nc.dram_tensor("h_table", [BLOCKS * P, F], fp32).ap()
    y_table = nc.dram_tensor("y_table", [BLOCKS * P, ROW], fp32).ap()
    edge_list = nc.dram_tensor("edge_list", [P * NTL, 2], i32).ap()
    messages = nc.dram_tensor("messages", [P * NT2, ROW], fp32).ap()
    tile_block_dram = [nc.dram_tensor(f"tile_block_dram{n}", [NTB], i32).ap() for n in range(2)]

    with ctx:
        lane_row = sbuf(ctx, "lane_row", [P, P])
        part = sbuf(ctx, "part", [P, 1])
        ident = sbuf(ctx, "ident", [P, P])
        before = sbuf(ctx, "before", [P, P])
        ones = sbuf(ctx, "ones", [P, P])
        zeros = sbuf(ctx, "zeros", [P, ZROW])
        x_nodes = sbuf(ctx, "x_nodes", [P, NBP, F])
        h_nodes = sbuf(ctx, "h_nodes", [P, NBP, 2 * F])
        y_nodes = sbuf(ctx, "y_nodes", [P, NBP, ROW])
        r_deg = sbuf(ctx, "r_deg", [P, BLOCKS])
        deg_sum = sbuf(ctx, "deg_sum", [P, BLOCKS])
        tile_block = sbuf(ctx, "tile_block", [1, NTB], i32)
        w1 = sbuf(ctx, "w1", [P, GROUP, HID1])
        w2 = sbuf(ctx, "w2", [HID1, 2 * F])
        b1c = sbuf(ctx, "b1c", [HID1, 1])
        b2r = sbuf(ctx, "b2r", [P, F])
        v1 = sbuf(ctx, "v1", [P, GROUP, P])
        v1c = sbuf(ctx, "v1c", [P, 1])
        v2 = sbuf(ctx, "v2", [P, 2 * F])
        v2r = sbuf(ctx, "v2r", [P, 2 * F])

        s_vec = sem("s_vec")
        vec_n = [0]

        s_const, s_fill, s_load, s_w = sem("s_const"), sem("s_fill"), sem("s_load"), sem("s_w")
        raw = ExitStack()
        src_raw = sbuf(raw, "src_raw", [P, NT0], i32)
        dst_raw = sbuf(raw, "dst_raw", [P, NT0], i32)
        setup = ExitStack()
        list_fill = sbuf(setup, "list_fill", [P, NTL // FILLS, 2], i32)
        with nc.Block() as block:
            @block.gpsimd
            def _(pool):
                nc.gpsimd.iota(lane_row[:, :], [[1, P]], base=0, channel_multiplier=0,
                               allow_small_or_imprecise_dtypes=True)
                nc.gpsimd.iota(part[:, :], [[1, 1]], base=0, channel_multiplier=1,
                               allow_small_or_imprecise_dtypes=True).then_inc(s_const, 1)

            @block.vector
            def _(dve):
                chain = Chain(dve, s_vec)
                nc.vector.memset(zeros[:, :], 0.0)
                nc.vector.memset(ones[:, :], 1.0)
                nc.vector.memset(v2[:, :], 0.0)
                nc.vector.memset(w1[:, :, :], 0.0)
                nc.vector.memset(v1[:, :, :], 0.0)
                nc.vector.memset(y_nodes[:, :, :], 0.0)
                nc.vector.memset(x_nodes[:, :, :], 0.0)
                nc.vector.memset(src_raw[:, :], PAD_NODE)
                nc.vector.memset(dst_raw[:, :], PAD_NODE)
                nc.vector.memset(list_fill[:, :, 1], NO_LANE)
                chain(nc.vector.memset(list_fill[:, :, 0], PAD_NODE))
                dve.sem_inc(s_fill)
                dve.wait_ge(s_const, 1)
                nc.vector.tensor_scalar(ident[:, :], lane_row[:, :], part[:, 0:1], None, ALU.is_equal)
                chain(nc.vector.tensor_scalar(before[:, :], lane_row[:, :], part[:, 0:1], None, ALU.is_gt))
                vec_n[0] = chain.n

            @block.sync
            def _(sp):
                sp.wait_ge(s_fill, 1)
                lists = edge_list.rearrange("(p t) w -> p t w", p=P)
                for j in range(FILLS):
                    sp.dma_start(lists[:, j * (NTL // FILLS):(j + 1) * (NTL // FILLS), :], list_fill[:, :, :]
                                 ).then_inc(s_load, 16)
                sp.dma_start(x_table[0:NODES, :], x).then_inc(s_load, 16)
                sp.dma_start(x_table[NODES:, :], zeros[0:BLOCKS * P - NODES, 0:F]).then_inc(s_load, 16)
                full = EDGES // NT0
                for raw_sb, given in ((src_raw, src), (dst_raw, dst)):
                    sp.dma_start(raw_sb[0:full, :], given[0:full * NT0].rearrange("(p t) -> p t", p=full)
                                 ).then_inc(s_load, 16)
                    sp.dma_start(raw_sb[full:full + 1, 0:EDGES - full * NT0],
                                 given[full * NT0:EDGES].rearrange("(p t) -> p t", p=1)).then_inc(s_load, 16)
                whole = NODES // P
                sp.dma_start(x_nodes[:, 0:whole, :], x[0:whole * P, :].rearrange("(b l) f -> l b f", l=P)
                             ).then_inc(s_load, 16)
                sp.dma_start(x_nodes[0:NODES - whole * P, whole, :], x[whole * P:NODES, :]).then_inc(s_load, 16)
                sp.wait_ge(s_load, 16 * (FILLS + 8))

            @block.scalar
            def _(act):
                n = 0
                act.wait_ge(s_fill, 1)
                v1t = V1.rearrange("h k -> k h")
                loads = [(w2[:, 0:F], W2l), (w2[:, F:2 * F], W2r), (b1c[:, :], b1.rearrange("(h o) -> h o", o=1)),
                         (b2r[:, :], b2.partition_broadcast(P)),
                         (v1c[0:HID2, :], c1.rearrange("(h o) -> h o", o=1)),
                         (v1c[HID2:P, :], c1.rearrange("(h o) -> h o", o=1)),
                         (v2[0:HID2, 0:F], V2.rearrange("d h -> h d")),
                         (v2[HID2:P, F:2 * F], V2.rearrange("d h -> h d")),
                         (v2r[:, 0:F], c2.partition_broadcast(P)), (v2r[:, F:2 * F], c2.partition_broadcast(P))]
                for g in range(GROUP):
                    r = 2 * F * g
                    loads += [(w1[r:r + F, g, :], W1l), (w1[r + F:r + 2 * F, g, :], W1r),
                              (v1[r:r + 2 * F, g, 0:HID2], v1t),
                              (v1[r:r + F, g, HID2:P], v1t[F:2 * F, :]), (v1[r + F:r + 2 * F, g, HID2:P], v1t[0:F, :])]
                with nc.allow_non_contiguous_dma("small weights, once"):
                    for to, of in loads:
                        act.dma_start(to, of).then_inc(s_w, 16)
                act.wait_ge(s_w, 16 * len(loads))
        setup.close()

        def rank(tag, block_of, ncols, address, pitch, table, table_dram):
            s_hist, s_ps, s_tab = sem(f"s_hist{tag}"), sem(f"s_ps{tag}"), sem(f"s_tab{tag}")
            s_rtick = sem(f"s_rtick{tag}")
            s_h, s_r = sem(f"s_h{tag}"), sem(f"s_r{tag}")
            own = ExitStack()
            mask = sbuf(own, f"mask{tag}", [P, ncols])
            count = sbuf(own, f"count{tag}", [P, ncols])
            slot = sbuf(own, f"slot{tag}", [P, ncols])
            hist = sbuf(own, f"hist{tag}", [P, BLOCKS])
            first = sbuf(own, f"first{tag}", [P, BLOCKS])
            tiles = sbuf(own, f"tiles{tag}", [P, BLOCKS])
            ends = sbuf(own, f"ends{tag}", [P, BLOCKS])
            itmp = sbuf(own, f"itmp{tag}", [P, BLOCKS], i32)
            tile_no = sbuf(own, f"tile_no{tag}", [P, NTB // P])
            over = sbuf(own, f"over{tag}", [P, NTB // P, BLOCKS])
            tb = sbuf(own, f"tb{tag}", [P, NTB // P])
            tbi = sbuf(own, f"tbi{tag}", [P, NTB // P], i32)
            both = view(banks(own, f"both{tag}")[:, 0, :], 2, BLOCKS)
            with nc.Block() as block:
                @block.gpsimd
                def _(pool):
                    nc.gpsimd.iota(tile_no[:, :], [[1, NTB // P]], base=0, channel_multiplier=NTB // P,
                                   allow_small_or_imprecise_dtypes=True).then_inc(s_tab, 1)

                @block.tensor
                def _(pe):
                    pe.wait_ge(s_hist, 1)
                    nc.tensor.matmul(both[:, 0, :], ones[:, :], hist[:, :], start=True, stop=True)
                    nc.tensor.matmul(both[:, 1, :], before[:, :], hist[:, :], start=True, stop=True
                                     ).then_inc(s_ps, 1)

                @block.vector
                def _(dve):
                    chain_h = Chain(dve, s_h)
                    dve.sem_inc(s_h)
                    with dve.Fori(0, BLOCKS) as h:
                        dve.wait_ge(s_h, h + 1)
                        nc.vector.tensor_scalar(mask[:, :], block_of, lane_row[:, bass.ds(h, 1)], 0.0,
                                                ALU.is_equal, ALU.add, accum_out=hist[:, bass.ds(h, 1)]
                                                ).then_inc(s_h, 1)
                    dve.wait_ge(s_h, BLOCKS + 1)
                    dve.sem_inc(s_hist)
                    chain = Chain(dve, s_vec)
                    chain.n = vec_n[0]
                    dve.wait_ge(s_ps, 1)
                    chain(nc.vector.tensor_scalar(tiles[:, :], both[:, 0, :], float(P - 1), None, ALU.add))
                    chain(nc.vector.tensor_copy(itmp[:, :], tiles[:, :]))
                    chain(nc.vector.tensor_scalar(itmp[:, :], itmp[:, :], 7, None, ALU.logical_shift_right))
                    chain(nc.vector.tensor_copy(tiles[:, :], itmp[:, :]))
                    chain(nc.vector.tensor_tensor_scan(ends[:, :], tiles[:, :], zeros[:, 0:BLOCKS], 0.0,
                                                       ALU.add, ALU.add))
                    chain(nc.vector.tensor_tensor(first[:, :], ends[:, :], tiles[:, :], ALU.subtract))
                    chain(nc.vector.tensor_scalar(first[:, :], first[:, :], float(P), -1.0, ALU.mult, ALU.add))
                    chain(nc.vector.tensor_tensor(first[:, :], first[:, :], both[:, 1, :], ALU.add))
                    dve.wait_ge(s_tab, 1)
                    chain(nc.vector.tensor_tensor(
                        over[:, :, :], ends[:, :].unsqueeze(1).to_broadcast([P, NTB // P, BLOCKS]),
                        tile_no[:, :].unsqueeze(2).to_broadcast([P, NTB // P, BLOCKS]), ALU.is_le))
                    chain(nc.vector.tensor_reduce(tb[:, :], over[:, :, :], AX, ALU.add))
                    chain(nc.vector.tensor_scalar(tb[:, :], tb[:, :], float(BLOCKS - 1), None, ALU.min))
                    nc.vector.tensor_copy(tbi[:, :], tb[:, :]).then_inc(s_tab, 1)
                    vec_n[0] = chain.n
                    steps = Chain(dve, s_r)
                    with dve.Fori(0, BLOCKS) as h:
                        steps.turn(h, 3)
                        steps(nc.vector.tensor_scalar(mask[:, :], block_of, lane_row[:, bass.ds(h, 1)], None,
                                                      ALU.is_equal))
                        steps(nc.vector.tensor_tensor_scan(count[:, :], mask[:, :], mask[:, :],
                                                           first[:, bass.ds(h, 1)], ALU.add, ALU.max))
                        dve.sem_inc(s_rtick)
                        steps(nc.vector.copy_predicated(slot[:, :], mask[:, :].bitcast(i32), count[:, :]))
                    chain = Chain(dve, s_vec)
                    chain.n = vec_n[0]
                    chain(nc.vector.tensor_copy(address, slot[:, :]))
                    chain(nc.vector.tensor_scalar(address, address, P - 1, None, ALU.bitwise_and))
                    chain(nc.vector.tensor_copy(count[:, :], address))
                    chain(nc.vector.tensor_copy(address, slot[:, :]))
                    chain(nc.vector.tensor_scalar(address, address, 7, None, ALU.logical_shift_right))
                    chain(nc.vector.tensor_copy(mask[:, :], address))
                    chain(nc.vector.scalar_tensor_tensor(mask[:, :], count[:, :], float(pitch), mask[:, :],
                                                         ALU.mult, ALU.add))
                    chain(nc.vector.tensor_copy(address, mask[:, :]))
                    vec_n[0] = chain.n

                @block.sync
                def _(sp):
                    sp.wait_ge(s_tab, 2)
                    sp.dma_start(table_dram.rearrange("(p t) -> p t", p=P), tbi[:, :]).then_inc(s_tab, 16)
                    sp.wait_ge(s_tab, 18)
                    sp.dma_start(table[0:1, :], table_dram.rearrange("(o t) -> o t", o=1)).then_inc(s_tab, 16)
                    sp.wait_ge(s_tab, 34)
            own.close()

        order = ExitStack()
        address0 = sbuf(order, "address0", [P, NT0], i32)
        pair = sbuf(order, "pair", [P, NT0, 2], i32)
        dst_block = sbuf(order, "dst_block", [P, NT0])
        tmp_i = sbuf(order, "tmp_i", [P, NT0], i32)
        with nc.Block() as block:
            @block.vector
            def _(dve):
                chain = Chain(dve, s_vec)
                chain.n = vec_n[0]
                chain(nc.vector.tensor_scalar(tmp_i[:, :], dst_raw[:, :], 7, None, ALU.logical_shift_right))
                nc.vector.tensor_copy(dst_block[:, :], tmp_i[:, :])
                nc.vector.tensor_copy(pair[:, :, 0], src_raw[:, :])
                chain(nc.vector.tensor_scalar(pair[:, :, 1], dst_raw[:, :], P - 1, None, ALU.bitwise_and))
                vec_n[0] = chain.n
        rank("d", dst_block[:, :], NT0, address0[:, :], NTL, tile_block, tile_block_dram[0])

        s_pay, s_put = sem("s_pay"), [sem(f"s_put{b}") for b in range(2)]
        s_ptick = sem("s_ptick")
        pay_i = sbuf(order, "pay_i", [P, 2, CH], i32)
        pay_v = sbuf(order, "pay_v", [P, 2, CH, 2], i32)
        with nc.Block() as block:
            @block.scalar
            def _(act):
                def payload(at, b):
                    nc.scalar.copy(pay_i[:, b, :], address0[:, bass.ds(at + b * CH, CH)])
                    nc.scalar.copy(pay_v[:, b, :, :], pair[:, bass.ds(at + b * CH, CH), :]).then_inc(s_pay, 1)
                for b in range(2):
                    payload(0, b)
                with act.Fori(1, NT0 // PAIR) as i:
                    for b in range(2):
                        act.wait_ge(s_put[b], i * (16 * CH))
                        act.sem_inc(s_ptick)
                        payload(i * PAIR, b)

            @block.gpsimd
            def _(pool):
                with pool.Fori(0, NT0 // PAIR) as i:
                    for b in range(2):
                        pool.wait_ge(s_pay, i * 2 + (b + 1))
                        pool.sem_inc(s_ptick)
                        for k in range(CH):
                            pool.indirect_dma_start(
                                out=edge_list, out_offset=bass.IndirectOffsetOnAxis(ap=pay_i[:, b, k:k + 1], axis=0),
                                in_=pay_v[:, b, k, :], in_offset=None).then_inc(s_put[b], 16)
                for b in range(2):
                    pool.wait_ge(s_put[b], (NT0 // PAIR) * 16 * CH)
        order.close()
        raw.close()

        edges = sbuf(ctx, "edges", [P, NTL, 2], i32)
        dst_lane = sbuf(ctx, "dst_lane", [P, NTL], bf16)
        src_lane = sbuf(ctx, "src_lane", [P, NTL], bf16)
        src_block = sbuf(ctx, "src_block", [P, NTL], bf16)
        s_back = sem("s_back")
        split = ExitStack()
        tmp_e = sbuf(split, "tmp_e", [P, NTL], i32)
        with nc.Block() as block:
            @block.sync
            def _(sp):
                sp.dma_start(edges[:, :, :].rearrange("p t w -> p (t w)"),
                             edge_list.rearrange("(p t) w -> p (t w)", p=P)).then_inc(s_back, 16)

            @block.vector
            def _(dve):
                chain = Chain(dve, s_vec)
                chain.n = vec_n[0]
                dve.wait_ge(s_back, 16)
                nc.vector.tensor_copy(dst_lane[:, :], edges[:, :, 1])
                chain(nc.vector.tensor_scalar(tmp_e[:, :], edges[:, :, 0], P - 1, None, ALU.bitwise_and))
                chain(nc.vector.tensor_copy(src_lane[:, :], tmp_e[:, :]))
                chain(nc.vector.tensor_scalar(tmp_e[:, :], edges[:, :, 0], 7, None, ALU.logical_shift_right))
                chain(nc.vector.tensor_copy(src_block[:, :], tmp_e[:, :]))
                vec_n[0] = chain.n
        split.close()

        def one_hot(to, lanes, n, width=P):
            return nc.vector.tensor_tensor(to, lane_row[:, 0:width].unsqueeze(1).to_broadcast([P, n, width]),
                                           lanes.unsqueeze(2).to_broadcast([P, n, width]), ALU.is_equal)

        def blocks_of(tiles_from, engine):
            return nc.values_load_multi_w_load_instructions(
                tile_block[0:1, bass.ds(tiles_from, CH)], engines=[engine], min_val=0, max_val=BLOCKS - 1,
                skip_runtime_bounds_check_because="the table of tiles' blocks is clamped to the last block")[1]

        def add_tiles(tiles_from, parts, width):
            at = blocks_of(tiles_from, mybir.EngineType.DVE)
            for k in range(CH):
                to = acc[:, k, bass.ds(at[k], 1), 0:width].rearrange("p a f -> p (a f)")
                ins = nc.vector.tensor_tensor(to, to, parts[:, k, 0:width], ALU.add)
            return ins

        def merge(chain, width):
            for half in (4, 2, 1):
                chain(nc.vector.tensor_tensor(acc[:, 0:half, :, 0:width], acc[:, 0:half, :, 0:width],
                                              acc[:, half:2 * half, :, 0:width], ALU.add))

        def aggregate(tag, table, with_degrees):
            width = ROW if with_degrees else F
            s_idx, s_row = sem(f"s_idx{tag}"), [sem(f"s_row{tag}{b}") for b in range(2)]
            s_hot, s_mm, s_add = sem(f"s_hot{tag}"), sem(f"s_mm{tag}"), sem(f"s_add{tag}")
            s_tick, s_ready, s_zero = sem(f"s_tick{tag}"), sem(f"s_ready{tag}"), sem(f"s_zero{tag}")
            own = ExitStack()
            idx = sbuf(own, f"idx{tag}", [P, 2, CH], i32)
            rows = sbuf(own, f"rows{tag}", [P, 2, CH, ROW])
            hot = sbuf(own, f"hot{tag}", [P, 2, CH, P])
            sum_banks = banks(own, f"sum_banks{tag}", 2)
            sum_ps = [view(sum_banks[:, b, :], CH, ROW) for b in range(2)]
            if with_degrees:
                hot_sl = sbuf(own, f"hot_sl{tag}", [P, 2, CH, P], bf16)
                hot_sb = sbuf(own, f"hot_sb{tag}", [P, 2, CH, P], bf16)
                deg_ps = banks(own, f"deg_ps{tag}")[:, 0, 0:P]
            turns = NT1 // PAIR
            with nc.Block() as block:
                @block.scalar
                def _(act):
                    for b in range(2):
                        nc.scalar.copy(idx[:, b, :], edges[:, b * CH:(b + 1) * CH, 0]).then_inc(s_idx, 1)
                    with act.Fori(0, turns) as i:
                        for b in range(2):
                            act.wait_ge(s_row[b], i * (16 * CH) + 16 * CH)
                            act.sem_inc(s_tick)
                            nc.scalar.copy(idx[:, b, :], edges[:, bass.ds(i * PAIR + (PAIR + b * CH), CH), 0]
                                           ).then_inc(s_idx, 1)

                @block.gpsimd
                def _(pool):
                    def gather(b):
                        for k in range(CH):
                            pool.indirect_dma_start(
                                out=rows[:, b, k, 0:F], out_offset=None, in_=table,
                                in_offset=bass.IndirectOffsetOnAxis(ap=idx[:, b, k:k + 1], axis=0)
                            ).then_inc(s_row[b], 16)
                    nc.gpsimd.memset(rows[:, :, :, F:ROW], 1.0).then_inc(s_ready, 1)
                    for b in range(2):
                        pool.wait_ge(s_idx, b + 1)
                        gather(b)
                    with pool.Fori(0, turns) as i:
                        for b in range(2):
                            pool.wait_ge(s_idx, i * 2 + (b + 3))
                            pool.wait_ge(s_mm, i * 2 + (b + 3))
                            pool.sem_inc(s_tick)
                            gather(b)
                    for b in range(2):
                        pool.wait_ge(s_row[b], (turns + 1) * 16 * CH)

                @block.vector
                def _(dve):
                    dve.sem_inc(s_add)
                    nc.vector.memset(acc[:, :, :, :], 0.0).then_inc(s_add, 1)
                    with dve.Fori(0, turns) as i:
                        for b in range(2):
                            dve.wait_ge(s_mm, i * 2 + (b + 1))
                            last = one_hot(hot[:, b, :, :], dst_lane[:, bass.ds(i * PAIR + b * CH, CH)], CH)
                            if with_degrees:
                                one_hot(hot_sl[:, b, :, :], src_lane[:, bass.ds(i * PAIR + b * CH, CH)], CH)
                                last = one_hot(hot_sb[:, b, :, :], src_block[:, bass.ds(i * PAIR + b * CH, CH)], CH)
                            last.then_inc(s_hot, 1)
                        for b in range(2):
                            dve.wait_ge(s_mm, i * 2 + (b + 3))
                            dve.wait_ge(s_add, i * 2 + (b + 2))
                            add_tiles(i * PAIR + b * CH, sum_ps[b], width).then_inc(s_add, 1)
                    chain = Chain(dve, s_vec)
                    chain.n = vec_n[0]
                    dve.wait_ge(s_add, 2 * turns + 2)
                    merge(chain, width)
                    if with_degrees:
                        chain(nc.vector.tensor_tensor(deg_sum[:, :], acc[:, 0, :, F], deg_ps[:, 0:BLOCKS], ALU.add))
                    vec_n[0] = chain.n

                @block.tensor
                def _(pe):
                    pe.sem_inc(s_mm, 2)
                    pe.wait_ge(s_ready, 1)
                    if with_degrees:
                        nc.tensor.matmul(deg_ps[:, :], zeros[:, 0:P], zeros[:, 0:P], start=True, stop=True)
                    with pe.Fori(0, turns) as i:
                        for b in range(2):
                            pe.wait_ge(s_row[b], i * (16 * CH) + 16 * CH)
                            pe.wait_ge(s_hot, i * 2 + (b + 1))
                            pe.wait_ge(s_add, i * 2 + (b + 1))
                            pe.sem_inc(s_tick)
                            if with_degrees:
                                for k in range(CH):
                                    nc.tensor.matmul(deg_ps[:, :], hot_sl[:, b, k, :], hot_sb[:, b, k, :],
                                                     start=False, stop=True, skip_group_check=True)
                            for k in range(CH):
                                last = nc.tensor.matmul(sum_ps[b][:, k, 0:width], hot[:, b, k, :],
                                                        rows[:, b, k, 0:width], start=True, stop=True)
                            last.then_inc(s_mm, 1)

                if with_degrees:
                    @block.sync
                    def _(sp):
                        m = messages.rearrange("(p t) w -> p (t w)", p=P)
                        n = NT2 * ROW // ZROW
                        for j in range(n):
                            sp.dma_start(m[:, j * ZROW:(j + 1) * ZROW], zeros[:, :]).then_inc(s_mfill, 16)
                        sp.wait_ge(s_mfill, 16 * n)
            own.close()

        s_mfill = sem("s_mfill")
        sums = ExitStack()
        acc = sbuf(sums, "acc", [P, CH, BLOCKS, ROW])
        assert NT2 * ROW % ZROW == 0
        aggregate("a", x_table, True)

        s_cat, s_node, s_nt, s_ht = sem("s_cat"), sem("s_node"), sem("s_nt"), sem("s_ht")
        s_node_go = sem("s_node_go")
        own = ExitStack()
        cat = sbuf(own, "cat", [P, NBP, 2 * F])
        stage = sbuf(own, "stage", [P, P])
        stage_t = sbuf(own, "stage_t", [P, P])
        hidden = sbuf(own, "hidden", [HID1, GROUP * P])
        stage_ps = banks(own, "stage_ps")[:, 0, 0:P]
        hidden_ps = banks(own, "hidden_ps")[0:HID1, 0, :]
        out_ps = view(banks(own, "out_ps")[:, 0, :], GROUP, 2 * F)
        STEPS = 7
        with nc.Block() as block:
            @block.vector
            def _(dve):
                chain = Chain(dve, s_vec)
                chain.n = vec_n[0]
                nc.vector.tensor_scalar(r_deg[:, :], acc[:, 0, :, F], 1.0, None, ALU.max)
                chain(nc.vector.memset(cat[:, BLOCKS:, 0:F], 0.0))
                nc.vector.tensor_copy(cat[:, :, F:2 * F], x_nodes[:, :, :])
                chain(nc.vector.reciprocal(r_deg[:, :], r_deg[:, :]))
                chain(nc.vector.tensor_tensor(cat[:, 0:BLOCKS, 0:F], acc[:, 0, :, 0:F],
                                              r_deg[:, :].unsqueeze(2).to_broadcast([P, BLOCKS, F]), ALU.mult))
                dve.sem_inc(s_cat)
                vec_n[0] = chain.n
                with dve.Fori(0, GROUPS) as g:
                    dve.wait_ge(s_node, g * STEPS + 6)
                    dve.sem_inc(s_nt)
                    nc.vector.tensor_copy(h_nodes[:, bass.ds(g * GROUP, GROUP), :], out_ps[:, :, :]
                                          ).then_inc(s_node, 1)
                dve.wait_ge(s_node, GROUPS * STEPS)

            @block.scalar
            def _(act):
                act.wait_ge(s_cat, 1)
                with act.Fori(0, GROUPS) as g:
                    act.wait_ge(s_node_go, g + 1)
                    act.sem_inc(s_nt)
                    nc.scalar.copy(stage[:, :], cat[:, bass.ds(g * GROUP, GROUP), :].rearrange("p b f -> p (b f)")
                                   ).then_inc(s_node, 1)
                    act.wait_ge(s_node, g * STEPS + 2)
                    act.sem_inc(s_nt)
                    nc.scalar.copy(stage_t[:, :], stage_ps[:, :]).then_inc(s_node, 1)
                    act.wait_ge(s_node, g * STEPS + 4)
                    act.sem_inc(s_nt)
                    nc.scalar.activation(hidden[:, :], hidden_ps[:, :], ACT.Relu, bias=b1c[:, 0:1]
                                         ).then_inc(s_node, 1)

            @block.tensor
            def _(pe):
                pe.sem_inc(s_node_go)
                with pe.Fori(0, GROUPS) as g:
                    pe.wait_ge(s_node, g * STEPS + 1)
                    pe.sem_inc(s_nt)
                    nc.tensor.transpose(stage_ps[:, :], stage[:, :], ident[:, :]).then_inc(s_node, 1)
                    pe.wait_ge(s_node, g * STEPS + 3)
                    pe.sem_inc(s_nt)
                    for j in range(GROUP):
                        last = nc.tensor.matmul(hidden_ps[:, j * P:(j + 1) * P], w1[:, j, :], stage_t[:, :],
                                                start=True, stop=True)
                    last.then_inc(s_node, 1)
                    pe.wait_ge(s_node, g * STEPS + 5)
                    pe.sem_inc(s_nt)
                    for j in range(GROUP):
                        last = nc.tensor.matmul(out_ps[:, j, :], hidden[:, j * P:(j + 1) * P], w2[:, :],
                                                start=True, stop=True)
                    last.then_inc(s_node, 1)
                    pe.wait_ge(s_node, g * STEPS + 7)
                    pe.sem_inc(s_node_go)

            @block.sync
            def _(sp):
                sp.wait_ge(s_node, GROUPS * STEPS)
                sp.dma_start(h_table.rearrange("(b l) f -> l b f", l=P), h_nodes[:, 0:BLOCKS, 0:F]).then_inc(s_ht, 16)
                sp.wait_ge(s_ht, 16)
        own.close()

        aggregate("b", h_table, False)

        own = ExitStack()
        t_sum = sbuf(own, "t_sum", [P, BLOCKS, F])
        t_sq = sbuf(own, "t_sq", [P, BLOCKS, F])
        t_mean = sbuf(own, "t_mean", [P, BLOCKS])
        t_var = sbuf(own, "t_var", [P, BLOCKS])
        t_deg = sbuf(own, "t_deg", [P, BLOCKS])
        s_sq, s_rt = sem("s_sq"), sem("s_rt")

        def wide(v):
            return v[:, :].unsqueeze(2).to_broadcast([P, BLOCKS, F])

        def layer_norm(dve, chain, to, turn):
            chain(nc.vector.tensor_reduce(t_mean[:, :], t_sum[:, :, :], AX, ALU.add))
            chain(nc.vector.tensor_scalar(t_mean[:, :], t_mean[:, :], 1.0 / F, None, ALU.mult))
            chain(nc.vector.tensor_tensor(t_sum[:, :, :], t_sum[:, :, :], wide(t_mean), ALU.subtract))
            chain(nc.vector.tensor_tensor(t_sq[:, :, :], t_sum[:, :, :], t_sum[:, :, :], ALU.mult))
            chain(nc.vector.tensor_reduce(t_var[:, :], t_sq[:, :, :], AX, ALU.add))
            chain(nc.vector.tensor_scalar(t_var[:, :], t_var[:, :], 1.0 / F, LN_EPS, ALU.mult, ALU.add))
            dve.sem_inc(s_sq)
            dve.wait_ge(s_rt, turn)
            chain(nc.vector.reciprocal(t_var[:, :], t_var[:, :]))
            chain(nc.vector.tensor_tensor(to, t_sum[:, :, :], wide(t_var), ALU.mult))

        s_y = sem("s_y")
        with nc.Block() as block:
            @block.vector
            def _(dve):
                chain = Chain(dve, s_vec)
                chain.n = vec_n[0]
                chain(nc.vector.tensor_scalar(t_deg[:, :], deg_sum[:, :], 1e-5, None, ALU.max))
                chain(nc.vector.tensor_tensor(t_sum[:, :, :], acc[:, 0, :, 0:F], wide(r_deg), ALU.mult))
                chain(nc.vector.tensor_tensor(t_sum[:, :, :], t_sum[:, :, :], h_nodes[:, 0:BLOCKS, F:2 * F], ALU.add))
                chain(nc.vector.tensor_tensor(t_sum[:, :, :], t_sum[:, :, :],
                                              b2r[:, :].unsqueeze(1).to_broadcast([P, BLOCKS, F]), ALU.add))
                chain(nc.vector.tensor_tensor(t_sum[:, :, :], t_sum[:, :, :], x_nodes[:, 0:BLOCKS, :], ALU.add))
                layer_norm(dve, chain, y_nodes[:, 0:BLOCKS, 0:F], 2)
                chain(nc.vector.reciprocal(y_nodes[:, 0:BLOCKS, F], t_deg[:, :]))
                dve.sem_inc(s_y)
                vec_n[0] = chain.n

            @block.scalar
            def _(act):
                act.wait_ge(s_sq, 1)
                nc.scalar.sqrt(t_deg[:, :], t_deg[:, :]).then_inc(s_rt, 1)
                nc.scalar.sqrt(t_var[:, :], t_var[:, :]).then_inc(s_rt, 1)

            @block.sync
            def _(sp):
                sp.wait_ge(s_y, 1)
                sp.dma_start(y_table.rearrange("(b l) f -> l b f", l=P), y_nodes[:, 0:BLOCKS, :]).then_inc(s_y, 16)
                sp.wait_ge(s_y, 17)
        own.close()

        sums.close()

        order = ExitStack()
        address1 = sbuf(order, "address1", [P, NT1], i32)
        tile_block2 = sbuf(order, "tile_block2", [1, NTB], i32)
        rank("s", src_block[:, 0:NT1], NT1, address1[:, :], NT2, tile_block2, tile_block_dram[1])

        acc = sbuf(order, "acc_sheaf", [P, CH, BLOCKS, ROW])
        s_idx, s_adr, s_msg = sem("s_idx3"), sem("s_adr3"), sem("s_msg3")
        s_row = [sem(f"s_row3{b}") for b in range(2)]
        s_put = [sem(f"s_put3{b}") for b in range(2)]
        s_hot, s_hott, s_hotc, s_ownr = sem("s_hot3"), sem("s_hott"), sem("s_hotc"), sem("s_own3")
        s_xc, s_xt, s_xtc, s_hid, s_hidr, s_map = (sem(n) for n in ("s_xc", "s_xt", "s_xtc", "s_hid", "s_hidr", "s_map"))
        s_free = sem("s_free")
        s_msg2 = sem("s_msg2")
        s_mapu, s_mm, s_add, s_tick, s_d = (sem(n) for n in ("s_mapu", "s_mm3", "s_add3", "s_tick3", "s_d3"))
        own = ExitStack()
        idx = sbuf(own, "idx3", [P, 2, CH], i32)
        adr = sbuf(own, "adr3", [P, 2, CH], i32)
        rows = sbuf(own, "rows3", [P, 2, CH, ROW])
        hot = sbuf(own, "hot3", [P, 2, CH, P])
        hot_t = sbuf(own, "hot_t", [P, CH, P])
        xx = sbuf(own, "xx", [P, 2, CH, 2, F])
        inv = sbuf(own, "inv", [P, 2, 2, CH])
        xx_t = sbuf(own, "xx_t", [P, 2, P])
        hid = sbuf(own, "hid", [P, CH, P])
        v = sbuf(own, "v", [P, CH, 2, F])
        t = sbuf(own, "t", [P, CH, 2, F])
        t2 = sbuf(own, "t2", [P, CH, 2, F])
        w = sbuf(own, "w", [P, CH, 2, F])
        n2 = sbuf(own, "n2", [P, CH, 2])
        d = sbuf(own, "d", [P, CH, 2])
        msg_s = sbuf(own, "msg_s", [P, 2, CH, ROW])
        msg_d = sbuf(own, "msg_d", [P, CH, F])
        hot_ps = banks(own, "hot_ps", 2)[:, :, :].rearrange("p a (k l) -> p (a k) l", l=P)
        own_ps = view(banks(own, "own_ps")[:, 0, :], CH, ROW)
        xx_ps = view(banks(own, "xx_ps")[:, 0, :], 2, P)
        hid_ps = banks(own, "hid_ps", 2)[:, :, :].rearrange("p a (k l) -> p (a k) l", l=P)
        map_ps = view(banks(own, "map_ps")[:, 0, :], CH, 2 * F)
        sum_ps = view(banks(own, "sum_ps3")[:, 0, :], CH, F)
        turns = NT1 // PAIR
        DSTEPS = 14
        with nc.Block() as block:
            @block.gpsimd
            def _(pool):
                def gather(b):
                    for k in range(CH):
                        pool.indirect_dma_start(
                            out=rows[:, b, k, :], out_offset=None, in_=y_table,
                            in_offset=bass.IndirectOffsetOnAxis(ap=idx[:, b, k:k + 1], axis=0)
                        ).then_inc(s_row[b], 16)
                pool.sem_inc(s_free, 2)
                for b in range(2):
                    pool.wait_ge(s_idx, b + 1)
                    gather(b)
                with pool.Fori(0, turns) as i:
                    for b in range(2):
                        pool.wait_ge(s_msg, i * 2 + (b + 1))
                        pool.wait_ge(s_adr, i * 2 + (b + 1))
                        pool.wait_ge(s_xc, i * 2 + (b + 1))
                        pool.wait_ge(s_idx, i * 2 + (b + 3))
                        pool.sem_inc(s_tick)
                        for k in range(CH):
                            pool.indirect_dma_start(
                                out=messages, out_offset=bass.IndirectOffsetOnAxis(ap=adr[:, b, k:k + 1], axis=0),
                                in_=msg_s[:, b, k, :], in_offset=None).then_inc(s_put[b], 16)
                        gather(b)
                        pool.wait_ge(s_put[b], i * (16 * CH) + 16 * CH)
                        pool.sem_inc(s_free)
                for b in range(2):
                    pool.wait_ge(s_row[b], (turns + 1) * 16 * CH)

            @block.scalar
            def _(act):
                def copy_hot(c):
                    act.wait_ge(s_hott, c + 1)
                    act.sem_inc(s_tick)
                    for half in range(2):
                        last = nc.scalar.copy(hot_t[:, half * 4:half * 4 + 4, :], hot_ps[:, half * 4:half * 4 + 4, :])
                    last.then_inc(s_hotc, 1)
                for b in range(2):
                    nc.scalar.copy(idx[:, b, :], edges[:, b * CH:(b + 1) * CH, 0]).then_inc(s_idx, 1)
                copy_hot(0)
                with act.Fori(0, turns) as i:
                    for b in range(2):
                        c = i * 2 + b
                        act.wait_ge(s_row[b], i * (16 * CH) + 16 * CH)
                        act.wait_ge(s_ownr, c + 1)
                        act.wait_ge(s_msg2, c + 1)
                        act.sem_inc(s_tick)
                        nc.scalar.copy(xx[:, b, :, 0, :], rows[:, b, :, 0:F])
                        nc.scalar.copy(xx[:, b, :, 1, :], own_ps[:, :, 0:F])
                        nc.scalar.copy(inv[:, b, 0, :], rows[:, b, :, F])
                        nc.scalar.copy(inv[:, b, 1, :], own_ps[:, :, F]).then_inc(s_xc, 1)
                        nc.scalar.copy(idx[:, b, :], edges[:, bass.ds(i * PAIR + (PAIR + b * CH), CH), 0]
                                       ).then_inc(s_idx, 1)
                        act.wait_ge(s_xt, c + 1)
                        act.sem_inc(s_tick)
                        nc.scalar.copy(xx_t[:, :, :], xx_ps[:, :, :]).then_inc(s_xtc, 1)
                        act.wait_ge(s_hid, c + 1)
                        act.sem_inc(s_tick)
                        for half in range(2):
                            last = nc.scalar.activation(hid[:, half * 4:half * 4 + 4, :],
                                                        hid_ps[:, half * 4:half * 4 + 4, :], ACT.Relu,
                                                        bias=v1c[:, 0:1])
                        last.then_inc(s_hidr, 1)
                        act.wait_ge(s_free, c + 1)
                        act.sem_inc(s_tick)
                        nc.scalar.copy(msg_s[:, b, :, F], src_lane[:, bass.ds(i * PAIR + b * CH, CH)])
                        nc.scalar.copy(adr[:, b, :], address1[:, bass.ds(i * PAIR + b * CH, CH)]).then_inc(s_adr, 1)
                        copy_hot(c + 1)

            @block.tensor
            def _(pe):
                def own_rows(c, b, at):
                    pe.wait_ge(s_hot, c + 1)
                    pe.sem_inc(s_tick)
                    for k in range(CH):
                        last = nc.tensor.transpose(hot_ps[:, k, :], hot[:, b, k, :], ident[:, :])
                    last.then_inc(s_hott, 1)
                    blocks = blocks_of(at, mybir.EngineType.PE)
                    pe.wait_ge(s_hotc, c + 1)
                    pe.sem_inc(s_tick)
                    for k in range(CH):
                        last = nc.tensor.matmul(own_ps[:, k, :], hot_t[:, k, :],
                                                y_nodes[:, bass.ds(blocks[k], 1), :].rearrange("p a f -> p (a f)"),
                                                start=True, stop=True)
                    last.then_inc(s_ownr, 1)
                own_rows(0, 0, 0)
                with pe.Fori(0, turns) as i:
                    for b in range(2):
                        c = i * 2 + b
                        pe.wait_ge(s_xc, c + 1)
                        pe.sem_inc(s_tick)
                        for g in range(2):
                            last = nc.tensor.transpose(
                                xx_ps[:, g, :], xx[:, b, 4 * g:4 * g + 4, :, :].rearrange("p k e f -> p (k e f)"),
                                ident[:, :])
                        last.then_inc(s_xt, 1)
                        pe.wait_ge(s_xtc, c + 1)
                        pe.sem_inc(s_tick)
                        for k in range(CH):
                            last = nc.tensor.matmul(hid_ps[:, k, :], v1[:, k % GROUP, :], xx_t[:, k // GROUP, :],
                                                    start=True, stop=True)
                        last.then_inc(s_hid, 1)
                        pe.wait_ge(s_hidr, c + 1)
                        pe.wait_ge(s_mapu, c + 1)
                        pe.sem_inc(s_tick)
                        for k in range(CH):
                            last = nc.tensor.matmul(map_ps[:, k, :], hid[:, k, :], v2[:, :], start=True, stop=True)
                        last.then_inc(s_map, 1)
                        own_rows(c + 1, 1 - b, i * PAIR + (b + 1) * CH)
                        pe.wait_ge(s_msg2, c + 2)
                        pe.sem_inc(s_tick)
                        for k in range(CH):
                            last = nc.tensor.matmul(sum_ps[:, k, :], hot[:, b, k, :], msg_d[:, k, :],
                                                    start=True, stop=True)
                        last.then_inc(s_mm, 1)

            @block.vector
            def _(dve):
                def pairs(x):
                    return x[:, :, :].unsqueeze(3).to_broadcast([P, CH, 2, F])

                dve.sem_inc(s_mapu)
                dve.sem_inc(s_msg2)
                nc.vector.memset(acc[:, :, :, :], 0.0).then_inc(s_add, 1)
                one_hot(hot[:, 0, :, :], dst_lane[:, 0:CH], CH).then_inc(s_hot, 1)
                steps = Chain(dve, s_d)
                with dve.Fori(0, turns) as i:
                    steps.turn(i, 2 * DSTEPS)
                    for b in range(2):
                        c = i * 2 + b
                        x_both = xx[:, b, :, :, :]
                        one_hot(hot[:, 1 - b, :, :], dst_lane[:, bass.ds(i * PAIR + (b + 1) * CH, CH)], CH
                                ).then_inc(s_hot, 1)
                        dve.wait_ge(s_map, c + 1)
                        steps(nc.vector.tensor_tensor(
                            v[:, :, :, :].rearrange("p k e f -> p k (e f)"), map_ps[:, :, :],
                            v2r[:, :].unsqueeze(1).to_broadcast([P, CH, 2 * F]), ALU.add))
                        dve.sem_inc(s_mapu)
                        nc.vector.tensor_tensor(t[:, :, :, :], v[:, :, :, :], v[:, :, :, :], ALU.mult)
                        steps(nc.vector.tensor_tensor(t2[:, :, :, :], v[:, :, :, :], x_both, ALU.mult))
                        nc.vector.tensor_reduce(d[:, :, :], t2[:, :, :, :], AX, ALU.add)
                        steps(nc.vector.tensor_reduce(n2[:, :, :], t[:, :, :, :], AX, ALU.add))
                        steps(nc.vector.tensor_scalar(n2[:, :, :], n2[:, :, :], NORM_EPS2, 0.5, ALU.max, ALU.mult))
                        steps(nc.vector.reciprocal(n2[:, :, :], n2[:, :, :]))
                        steps(nc.vector.tensor_tensor(d[:, :, :], d[:, :, :], n2[:, :, :], ALU.mult))
                        steps(nc.vector.tensor_tensor(t[:, :, :, :], v[:, :, :, :], pairs(d), ALU.mult))
                        nc.vector.tensor_tensor(w[:, :, 0, :], x_both[:, :, 1, :], t[:, :, 1, :], ALU.subtract)
                        steps(nc.vector.tensor_tensor(w[:, :, 1, :], x_both[:, :, 0, :], t[:, :, 0, :], ALU.subtract))
                        steps(nc.vector.tensor_tensor(t2[:, :, :, :], v[:, :, :, :], w[:, :, :, :], ALU.mult))
                        steps(nc.vector.tensor_reduce(d[:, :, :], t2[:, :, :, :], AX, ALU.add))
                        steps(nc.vector.tensor_tensor(d[:, :, :], d[:, :, :], n2[:, :, :], ALU.mult))
                        steps(nc.vector.tensor_tensor(t[:, :, :, :], v[:, :, :, :], pairs(d), ALU.mult))
                        steps(nc.vector.tensor_tensor(w[:, :, :, :], w[:, :, :, :], t[:, :, :, :], ALU.subtract))
                        nc.vector.tensor_tensor(msg_d[:, :, :], w[:, :, 1, :],
                                                inv[:, b, 0, :].unsqueeze(2).to_broadcast([P, CH, F]), ALU.mult)
                        dve.wait_ge(s_free, c + 1)
                        steps(nc.vector.tensor_tensor(msg_s[:, b, :, 0:F], w[:, :, 0, :],
                                                      inv[:, b, 1, :].unsqueeze(2).to_broadcast([P, CH, F]), ALU.mult))
                        dve.sem_inc(s_msg)
                        dve.sem_inc(s_msg2)
                        dve.wait_ge(s_mm, c + 1)
                        dve.wait_ge(s_add, c + 1)
                        add_tiles(i * PAIR + b * CH, sum_ps, F).then_inc(s_add, 1)
        own.close()

        own = ExitStack()
        DEEP = 4
        s_in = [sem(f"s_in{q}") for q in range(DEEP)]
        s_hot, s_mm, s_add2, s_tick = sem("s_hot4"), sem("s_mm4"), sem("s_add4"), sem("s_tick4")
        got = sbuf(own, "got", [P, DEEP, CH, ROW])
        hot = sbuf(own, "hot4", [P, 2, CH, P])
        sum_banks = banks(own, "sum_banks4", 2)
        sum_ps = [view(sum_banks[:, b, :], CH, F) for b in range(2)]
        m_rows = messages.rearrange("(p t) w -> p t w", p=P)
        turns4 = NT2 // (DEEP * CH)

        def add_sources(at_tile, parts):
            at = nc.values_load_multi_w_load_instructions(
                tile_block2[0:1, bass.ds(at_tile, CH)], engines=[mybir.EngineType.DVE], min_val=0, max_val=BLOCKS - 1,
                skip_runtime_bounds_check_because="the table of tiles' blocks is clamped to the last block")[1]
            for k in range(CH):
                to = acc[:, k, bass.ds(at[k], 1), 0:F].rearrange("p a f -> p (a f)")
                ins = nc.vector.tensor_tensor(to, to, parts[:, k, :], ALU.add)
            return ins

        with nc.Block() as block:
            @block.sync
            def _(sp):
                with sp.Fori(0, turns4) as i:
                    for q in range(DEEP):
                        sp.wait_ge(s_mm, i * DEEP + (q + 1))
                        sp.sem_inc(s_tick)
                        sp.dma_start(got[:, q, :, :], m_rows[:, bass.ds(i * (DEEP * CH) + q * CH, CH), :]
                                     ).then_inc(s_in[q], 16)

            @block.vector
            def _(dve):
                dve.sem_inc(s_add2, 2)
                with dve.Fori(0, turns4) as i:
                    for q0 in range(0, DEEP, 2):
                        for q in (q0, q0 + 1):
                            dve.wait_ge(s_in[q], i * 16 + 16)
                            dve.wait_ge(s_mm, i * DEEP + (q + 3))
                            dve.sem_inc(s_tick)
                            one_hot(hot[:, q % 2, :, :], got[:, q, :, F], CH).then_inc(s_hot, 1)
                        for q in (q0, q0 + 1):
                            dve.wait_ge(s_mm, i * DEEP + (q + 5))
                            dve.wait_ge(s_add2, i * DEEP + (q + 2))
                            add_sources(i * (DEEP * CH) + q * CH, sum_ps[q % 2]).then_inc(s_add2, 1)
                chain = Chain(dve, s_vec)
                chain.n = vec_n[0]
                dve.wait_ge(s_add2, NT2 // CH + 2)
                merge(chain, F)
                vec_n[0] = chain.n

            @block.tensor
            def _(pe):
                pe.sem_inc(s_mm, 4)
                with pe.Fori(0, turns4) as i:
                    for q in range(DEEP):
                        pe.wait_ge(s_in[q], i * 16 + 16)
                        pe.wait_ge(s_hot, i * DEEP + (q + 1))
                        pe.wait_ge(s_add2, i * DEEP + (q + 1))
                        pe.sem_inc(s_tick)
                        for k in range(CH):
                            last = nc.tensor.matmul(sum_ps[q % 2][:, k, :], hot[:, q % 2, k, :], got[:, q, k, 0:F],
                                                    start=True, stop=True)
                        last.then_inc(s_mm, 1)
        own.close()
        order.close()

        own = ExitStack()
        t_sum = sbuf(own, "t_sum5", [P, BLOCKS, F])
        t_sq = sbuf(own, "t_sq5", [P, BLOCKS, F])
        t_mean = sbuf(own, "t_mean5", [P, BLOCKS])
        t_var = sbuf(own, "t_var5", [P, BLOCKS])
        s_fin = sem("s_fin")
        y = y_nodes[:, 0:BLOCKS, 0:F]
        with nc.Block() as block:
            @block.vector
            def _(dve):
                chain = Chain(dve, s_vec)
                chain.n = vec_n[0]
                chain(nc.vector.tensor_tensor(t_sum[:, :, :], acc[:, 0, :, 0:F],
                                              y_nodes[:, 0:BLOCKS, F:ROW].to_broadcast([P, BLOCKS, F]), ALU.mult))
                chain(nc.vector.tensor_tensor(t_sum[:, :, :], t_sum[:, :, :], y, ALU.add))
                chain(nc.vector.tensor_scalar(t_sum[:, :, :], t_sum[:, :, :], 0.0, None, ALU.max))
                chain(nc.vector.tensor_tensor(t_sum[:, :, :], t_sum[:, :, :], y, ALU.add))
                layer_norm(dve, chain, t_sq[:, :, :], 3)
                dve.sem_inc(s_fin)

            @block.scalar
            def _(act):
                act.wait_ge(s_sq, 2)
                nc.scalar.sqrt(t_var[:, :], t_var[:, :]).then_inc(s_rt, 1)

            @block.sync
            def _(sp):
                sp.wait_ge(s_fin, 1)
                whole = NODES // P
                sp.dma_start(out[0:whole * P, :].rearrange("(b l) f -> l b f", l=P), t_sq[:, 0:whole, :]
                             ).then_inc(s_fin, 16)
                sp.dma_start(out[whole * P:NODES, :], t_sq[0:NODES - whole * P, whole, :]).then_inc(s_fin, 16)
                sp.wait_ge(s_fin, 33)
        own.close()


_INS = ['x', 'src', 'dst', 'L0_gnn_W1_l', 'L0_gnn_b1', 'L0_gnn_W1_r', 'L0_gnn_W2_l', 'L0_gnn_b2', 'L0_gnn_W2_r',
        'L1_gnn_W1', 'L1_gnn_b1', 'L1_gnn_W2', 'L1_gnn_b2']
_OUTS = [((NODES, F), 'float32')]


def kernel(**inputs):
    import numpy as _np
    import concourse.bacc as _bacc
    from concourse import mybir as _mybir
    from concourse.bass_utils import run_bass_kernel_spmd as _run

    nc = _bacc.Bacc("TRN2", target_bir_lowering=False, num_devices=1)
    arrays, args = {}, []
    for name in _INS:
        a = _np.ascontiguousarray(inputs[name])
        arrays[f"in_{name}_dram"] = a
        args.append(nc.dram_tensor(f"in_{name}_dram", a.shape, _mybir.dt.from_np(a.dtype), kind="ExternalInput").ap())
    for i, (shape, dtype) in enumerate(_OUTS):
        dt = _mybir.dt.from_np(_np.dtype(dtype))
        args.append(nc.dram_tensor(f"out_{i}_dram", shape, dt, kind="ExternalOutput").ap())
    gnn(nc, *args)
    r = _run(nc, [arrays], core_ids=[0])
    got = tuple(r.results[0][f"out_{i}_dram"] for i in range(len(_OUTS)))
    return got[0]
```

```python
import concourse.bass as bass
from concourse import mybir
from contextlib import ExitStack

fp32 = mybir.dt.float32
bf16 = mybir.dt.bfloat16
i32 = mybir.dt.int32
ALU = mybir.AluOpType
ACT = mybir.ActivationFunctionType
AX = mybir.AxisListType.X

P = 128
F = 16
NODES = 12500
EDGES = 412500
BLOCKS = -(-NODES // P)
PAD_NODE = BLOCKS * P - 1
GROUP = 4
GROUPS = -(-BLOCKS // GROUP)
NBP = GROUPS * GROUP
HID1, HID2 = 32, 64
CH = 8
PAIR = 2 * CH
QUAD = 4 * CH


def up(n, m):
    return -(-n // m) * m


NT0 = up(-(-EDGES // P), PAIR)
NT1 = up((NT0 * P + BLOCKS * (P - 1)) // P, QUAD)
NTL = NT1 + QUAD
NT2 = up((NT1 * P + BLOCKS * (P - 1)) // P, QUAD)
NTB = up(max(NTL, NT2), P)
HB = NT1 // QUAD
assert BLOCKS <= HB <= P
ROW = F + 1
PARTS = 3
MROW = (PARTS * F + 2) // 2
NO_LANE = 255

LN_EPS = 1e-5
BANK = 512
ZROW = BANK
FILLS = 8
NORM_EPS2 = 1e-24


class Chain:

    def __init__(self, eng, sem):
        self.eng, self.sem, self.n, self.base = eng, sem, 0, None

    def __call__(self, ins):
        ins.then_inc(self.sem, 1)
        self.n += 1
        self.eng.wait_ge(self.sem, self.n if self.base is None else self.base + self.n)

    def on(self, eng):
        self.eng = eng
        return self

    def turn(self, i, per_turn):
        self.base, self.n = i * per_turn, 0


def gnn(nc, x, src, dst, W1l, b1, W1r, W2l, b2, W2r, V1, c1, V2, c2, out):
    ctx = ExitStack()
    sems = {}

    def sem(name):
        sems[name] = ctx.enter_context(nc.semaphore(name))
        return sems[name]

    def sbuf(stack, name, shape, dt=fp32):
        return stack.enter_context(nc.sbuf_tensor(name, shape, dt))

    def banks(stack, name, n=1):
        return stack.enter_context(nc.psum_tensor(name, [P, n, BANK], fp32))

    def view(bank, n, m):
        return bank[:, 0:n * m].rearrange("p (n m) -> p n m", n=n)

    x_table = nc.dram_tensor("x_table", [BLOCKS * P, F], fp32).ap()
    h_table = nc.dram_tensor("h_table", [BLOCKS * P, F], fp32).ap()
    y_table = nc.dram_tensor("y_table", [BLOCKS * P, ROW], fp32).ap()
    edge_list = nc.dram_tensor("edge_list", [P * NTL, 2], i32).ap()
    messages = nc.dram_tensor("messages", [P * NT2, MROW], fp32).ap()
    tile_block_dram = [nc.dram_tensor(f"tile_block_dram{n}", [NTB], i32).ap() for n in range(2)]

    with ctx:
        lane_row = sbuf(ctx, "lane_row", [P, P])
        part = sbuf(ctx, "part", [P, 1])
        ident = sbuf(ctx, "ident", [P, P])
        ident_b = sbuf(ctx, "ident_b", [P, P], bf16)
        ones_b = sbuf(ctx, "ones_b", [P, 1], bf16)
        before = sbuf(ctx, "before", [P, P])
        ones = sbuf(ctx, "ones", [P, P])
        zeros = sbuf(ctx, "zeros", [P, ZROW])
        x_nodes = sbuf(ctx, "x_nodes", [P, NBP, F])
        h_nodes = sbuf(ctx, "h_nodes", [P, NBP, 2 * F])
        y_nodes = sbuf(ctx, "y_nodes", [P, NBP, ROW])
        y_parts = sbuf(ctx, "y_parts", [P, BLOCKS, PARTS, ROW], bf16)
        r_deg = sbuf(ctx, "r_deg", [P, BLOCKS])
        deg_sum = sbuf(ctx, "deg_sum", [P, BLOCKS])
        deg_dst = sbuf(ctx, "deg_dst", [P, BLOCKS])
        acc = sbuf(ctx, "acc", [P, CH, BLOCKS, F])
        hist = sbuf(ctx, "hist", [P, HB])
        first = sbuf(ctx, "first", [P, HB])
        tile_block = sbuf(ctx, "tile_block", [1, NTB], i32)
        w1 = sbuf(ctx, "w1", [P, GROUP, HID1])
        w2 = sbuf(ctx, "w2", [HID1, 2 * F])
        b1c = sbuf(ctx, "b1c", [HID1, 1])
        b2r = sbuf(ctx, "b2r", [P, F])
        v1 = sbuf(ctx, "v1", [P, GROUP, P])
        v1c = sbuf(ctx, "v1c", [P, 1])
        v2 = sbuf(ctx, "v2", [P, 2 * F])
        v2r = sbuf(ctx, "v2r", [P, 2 * F])

        s_vec = sem("s_vec")
        vec_chain = Chain(None, s_vec)

        s_const, s_fill, s_load, s_w = sem("s_const"), sem("s_fill"), sem("s_load"), sem("s_w")
        raw = ExitStack()
        src_raw = sbuf(raw, "src_raw", [P, NT0], i32)
        dst_raw = sbuf(raw, "dst_raw", [P, NT0], i32)
        setup = ExitStack()
        list_fill = sbuf(setup, "list_fill", [P, NTL // FILLS, 2], i32)
        with nc.Block() as block:
            @block.gpsimd
            def _(pool):
                nc.gpsimd.iota(lane_row[:, :], [[1, P]], base=0, channel_multiplier=0,
                               allow_small_or_imprecise_dtypes=True)
                nc.gpsimd.iota(part[:, :], [[1, 1]], base=0, channel_multiplier=1,
                               allow_small_or_imprecise_dtypes=True).then_inc(s_const, 1)

            @block.vector
            def _(dve):
                chain = vec_chain.on(dve)
                nc.vector.memset(zeros[:, :], 0.0)
                nc.vector.memset(ones[:, :], 1.0)
                nc.vector.memset(v2[:, :], 0.0)
                nc.vector.memset(w1[:, :, :], 0.0)
                nc.vector.memset(v1[:, :, :], 0.0)
                nc.vector.memset(y_nodes[:, :, :], 0.0)
                nc.vector.memset(x_nodes[:, :, :], 0.0)
                nc.vector.memset(src_raw[:, :], PAD_NODE)
                nc.vector.memset(dst_raw[:, :], PAD_NODE)
                nc.vector.memset(list_fill[:, :, 1], NO_LANE)
                chain(nc.vector.memset(list_fill[:, :, 0], PAD_NODE))
                dve.sem_inc(s_fill)
                dve.wait_ge(s_const, 1)
                nc.vector.memset(ones_b[:, :], 1.0)
                nc.vector.tensor_scalar(ident_b[:, :], lane_row[:, :], part[:, 0:1], None, ALU.is_equal)
                nc.vector.tensor_scalar(ident[:, :], lane_row[:, :], part[:, 0:1], None, ALU.is_equal)
                chain(nc.vector.tensor_scalar(before[:, :], lane_row[:, :], part[:, 0:1], None, ALU.is_gt))

            @block.sync
            def _(sp):
                sp.wait_ge(s_fill, 1)
                lists = edge_list.rearrange("(p t) w -> p t w", p=P)
                for j in range(FILLS):
                    sp.dma_start(lists[:, j * (NTL // FILLS):(j + 1) * (NTL // FILLS), :], list_fill[:, :, :]
                                 ).then_inc(s_load, 16)
                sp.dma_start(x_table[0:NODES, :], x).then_inc(s_load, 16)
                sp.dma_start(x_table[NODES:, :], zeros[0:BLOCKS * P - NODES, 0:F]).then_inc(s_load, 16)
                full = EDGES // NT0
                for raw_sb, given in ((src_raw, src), (dst_raw, dst)):
                    sp.dma_start(raw_sb[0:full, :], given[0:full * NT0].rearrange("(p t) -> p t", p=full)
                                 ).then_inc(s_load, 16)
                    sp.dma_start(raw_sb[full:full + 1, 0:EDGES - full * NT0],
                                 given[full * NT0:EDGES].rearrange("(p t) -> p t", p=1)).then_inc(s_load, 16)
                whole = NODES // P
                sp.dma_start(x_nodes[:, 0:whole, :], x[0:whole * P, :].rearrange("(b l) f -> l b f", l=P)
                             ).then_inc(s_load, 16)
                sp.dma_start(x_nodes[0:NODES - whole * P, whole, :], x[whole * P:NODES, :]).then_inc(s_load, 16)
                sp.wait_ge(s_load, 16 * (FILLS + 8))

            @block.scalar
            def _(act):
                n = 0
                act.wait_ge(s_fill, 1)
                v1t = V1.rearrange("h k -> k h")
                loads = [(w2[:, 0:F], W2l), (w2[:, F:2 * F], W2r), (b1c[:, :], b1.rearrange("(h o) -> h o", o=1)),
                         (b2r[:, :], b2.partition_broadcast(P)),
                         (v1c[0:HID2, :], c1.rearrange("(h o) -> h o", o=1)),
                         (v1c[HID2:P, :], c1.rearrange("(h o) -> h o", o=1)),
                         (v2[0:HID2, 0:F], V2.rearrange("d h -> h d")),
                         (v2[HID2:P, F:2 * F], V2.rearrange("d h -> h d")),
                         (v2r[:, 0:F], c2.partition_broadcast(P)), (v2r[:, F:2 * F], c2.partition_broadcast(P))]
                for g in range(GROUP):
                    r = 2 * F * g
                    loads += [(w1[r:r + F, g, :], W1l), (w1[r + F:r + 2 * F, g, :], W1r),
                              (v1[r:r + 2 * F, g, 0:HID2], v1t),
                              (v1[r:r + F, g, HID2:P], v1t[F:2 * F, :]), (v1[r + F:r + 2 * F, g, HID2:P], v1t[0:F, :])]
                with nc.allow_non_contiguous_dma("small weights, once"):
                    for to, of in loads:
                        act.dma_start(to, of).then_inc(s_w, 16)
                act.wait_ge(s_w, 16 * len(loads))
        setup.close()

        acc_flat = acc[:, :, :, :].rearrange("p k b f -> p (k b f)")
        count = acc_flat[:, 0:NT1]
        slot = acc_flat[:, NT1:2 * NT1]
        mask = acc_flat[:, 2 * NT1:2 * NT1 + NT1 // 2].bitcast(bf16)
        sums = acc_flat[:, 3 * NT1:3 * NT1 + BLOCKS * F].rearrange("p (b f) -> p b f", f=F)

        class Rank:

            def __init__(self, tag, block_of, n, address, pitch, table, table_dram):
                self.tag, self.block_of, self.n, self.address, self.pitch = tag, block_of, n, address, pitch
                self.table, self.table_dram = table, table_dram
                self.s_rtick = sem(f"s_rtick{tag}")
                self.s_hist, self.s_slot = sem(f"s_hist{tag}"), sem(f"s_slot{tag}")
                self.steps = Chain(None, self.s_slot)

            def count_block(self, dve, h):
                dve.wait_ge(self.s_hist, h + 1)
                nc.vector.tensor_scalar(mask[:, 0:self.n], self.block_of, lane_row[:, bass.ds(h, 1)], 0.0,
                                        ALU.is_equal, ALU.add, accum_out=hist[:, bass.ds(h, 1)]
                                        ).then_inc(self.s_hist, 1)

            def slots_of_block(self, h):
                self.steps.turn(h, 3)
                n = self.n
                return (
                    lambda dve: self.steps.on(dve)(nc.vector.tensor_scalar(
                        mask[:, 0:n], self.block_of, lane_row[:, bass.ds(h, 1)], None, ALU.is_equal)),
                    lambda dve: self.steps.on(dve)(nc.vector.tensor_tensor_scan(
                        count[:, 0:n], mask[:, 0:n], mask[:, 0:n], first[:, bass.ds(h, 1)], ALU.add, ALU.max)),
                    lambda dve: (dve.sem_inc(self.s_rtick), self.steps.on(dve)(nc.vector.copy_predicated(
                        slot[:, 0:n], mask[:, 0:n].bitcast(mybir.dt.int16), count[:, 0:n]))),
                )

            def place_blocks(self, counted):
                s_ps, s_tab = sem(f"s_ps{self.tag}"), sem(f"s_tab{self.tag}")
                own = ExitStack()
                tiles = sbuf(own, f"tiles{self.tag}", [P, HB])
                ends = sbuf(own, f"ends{self.tag}", [P, HB])
                itmp = sbuf(own, f"itmp{self.tag}", [P, HB], i32)
                tile_no = sbuf(own, f"tile_no{self.tag}", [P, NTB // P])
                over = sbuf(own, f"over{self.tag}", [P, NTB // P, BLOCKS])
                tb = sbuf(own, f"tb{self.tag}", [P, NTB // P])
                tbi = sbuf(own, f"tbi{self.tag}", [P, NTB // P], i32)
                both = view(banks(own, f"both{self.tag}")[:, 0, :], 2, HB)
                with nc.Block() as block:
                    @block.gpsimd
                    def _(pool):
                        nc.gpsimd.iota(tile_no[:, :], [[1, NTB // P]], base=0, channel_multiplier=NTB // P,
                                       allow_small_or_imprecise_dtypes=True).then_inc(s_tab, 1)

                    @block.tensor
                    def _(pe):
                        pe.wait_ge(self.s_hist, counted)
                        nc.tensor.matmul(both[:, 0, :], ones[:, :], hist[:, :], start=True, stop=True)
                        nc.tensor.matmul(both[:, 1, :], before[:, :], hist[:, :], start=True, stop=True
                                         ).then_inc(s_ps, 1)

                    @block.vector
                    def _(dve):
                        chain = vec_chain.on(dve)
                        dve.wait_ge(s_ps, 1)
                        chain(nc.vector.tensor_scalar(tiles[:, :], both[:, 0, :], float(P - 1), None, ALU.add))
                        chain(nc.vector.tensor_copy(itmp[:, :], tiles[:, :]))
                        chain(nc.vector.tensor_scalar(itmp[:, :], itmp[:, :], 7, None, ALU.logical_shift_right))
                        chain(nc.vector.tensor_copy(tiles[:, :], itmp[:, :]))
                        chain(nc.vector.tensor_tensor_scan(ends[:, :], tiles[:, :], zeros[:, 0:HB], 0.0,
                                                           ALU.add, ALU.add))
                        chain(nc.vector.tensor_tensor(first[:, :], ends[:, :], tiles[:, :], ALU.subtract))
                        chain(nc.vector.tensor_scalar(first[:, :], first[:, :], float(P), -1.0, ALU.mult, ALU.add))
                        chain(nc.vector.tensor_tensor(first[:, :], first[:, :], both[:, 1, :], ALU.add))
                        dve.wait_ge(s_tab, 1)
                        chain(nc.vector.tensor_tensor(
                            over[:, :, :], ends[:, 0:BLOCKS].unsqueeze(1).to_broadcast([P, NTB // P, BLOCKS]),
                            tile_no[:, :].unsqueeze(2).to_broadcast([P, NTB // P, BLOCKS]), ALU.is_le))
                        chain(nc.vector.tensor_reduce(tb[:, :], over[:, :, :], AX, ALU.add))
                        chain(nc.vector.tensor_scalar(tb[:, :], tb[:, :], float(BLOCKS - 1), None, ALU.min))
                        nc.vector.tensor_copy(tbi[:, :], tb[:, :]).then_inc(s_tab, 1)

                    @block.sync
                    def _(sp):
                        sp.wait_ge(s_tab, 2)
                        sp.dma_start(self.table_dram.rearrange("(p t) -> p t", p=P), tbi[:, :]).then_inc(s_tab, 16)
                        sp.wait_ge(s_tab, 18)
                        sp.dma_start(self.table[0:1, :], self.table_dram.rearrange("(o t) -> o t", o=1)
                                     ).then_inc(s_tab, 16)
                        sp.wait_ge(s_tab, 34)
                own.close()

            def addresses(self, chain):
                n, address = self.n, self.address
                chain(nc.vector.tensor_copy(address, slot[:, 0:n]))
                chain(nc.vector.tensor_scalar(address, address, P - 1, None, ALU.bitwise_and))
                chain(nc.vector.tensor_copy(count[:, 0:n], address))
                chain(nc.vector.tensor_copy(address, slot[:, 0:n]))
                chain(nc.vector.tensor_scalar(address, address, 7, None, ALU.logical_shift_right))
                chain(nc.vector.tensor_copy(slot[:, 0:n], address))
                chain(nc.vector.scalar_tensor_tensor(count[:, 0:n], count[:, 0:n], float(self.pitch), slot[:, 0:n],
                                                     ALU.mult, ALU.add))
                chain(nc.vector.tensor_copy(address, count[:, 0:n]))

        order = ExitStack()
        address0 = sbuf(order, "address0", [P, NT0], i32)
        pair = sbuf(order, "pair", [P, NT0, 2], i32)
        dst_block = sbuf(order, "dst_block", [P, NT0], bf16)
        with nc.Block() as block:
            @block.vector
            def _(dve):
                chain = vec_chain.on(dve)
                nc.vector.memset(hist[:, :], 0.0)
                chain(nc.vector.tensor_scalar(pair[:, :, 0], dst_raw[:, :], 7, None, ALU.logical_shift_right))
                chain(nc.vector.tensor_copy(dst_block[:, :], pair[:, :, 0]))
                nc.vector.tensor_copy(pair[:, :, 0], src_raw[:, :])
                chain(nc.vector.tensor_scalar(pair[:, :, 1], dst_raw[:, :], P - 1, None, ALU.bitwise_and))
        by_dst = Rank("d", dst_block[:, :], NT0, address0[:, :], NTL, tile_block, tile_block_dram[0])
        with nc.Block() as block:
            @block.vector
            def _(dve):
                dve.sem_inc(by_dst.s_hist)
                with dve.Fori(0, BLOCKS) as h:
                    by_dst.count_block(dve, h)
        by_dst.place_blocks(BLOCKS + 1)
        with nc.Block() as block:
            @block.vector
            def _(dve):
                with dve.Fori(0, BLOCKS) as h:
                    for step in by_dst.slots_of_block(h):
                        step(dve)
                by_dst.addresses(vec_chain.on(dve))

        s_pay, s_put = sem("s_pay"), [sem(f"s_put{b}") for b in range(2)]
        s_ptick = sem("s_ptick")
        pay_i = sbuf(order, "pay_i", [P, 2, CH], i32)
        pay_v = sbuf(order, "pay_v", [P, 2, CH, 2], i32)
        with nc.Block() as block:
            @block.scalar
            def _(act):
                def payload(at, b):
                    nc.scalar.copy(pay_i[:, b, :], address0[:, bass.ds(at + b * CH, CH)])
                    nc.scalar.copy(pay_v[:, b, :, :], pair[:, bass.ds(at + b * CH, CH), :]).then_inc(s_pay, 1)
                for b in range(2):
                    payload(0, b)
                with act.Fori(1, NT0 // PAIR) as i:
                    for b in range(2):
                        act.wait_ge(s_put[b], i * (16 * CH))
                        act.sem_inc(s_ptick)
                        payload(i * PAIR, b)

            @block.gpsimd
            def _(pool):
                with pool.Fori(0, NT0 // PAIR) as i:
                    for b in range(2):
                        pool.wait_ge(s_pay, i * 2 + (b + 1))
                        pool.sem_inc(s_ptick)
                        for k in range(CH):
                            pool.indirect_dma_start(
                                out=edge_list, out_offset=bass.IndirectOffsetOnAxis(ap=pay_i[:, b, k:k + 1], axis=0),
                                in_=pay_v[:, b, k, :], in_offset=None).then_inc(s_put[b], 16)
                for b in range(2):
                    pool.wait_ge(s_put[b], (NT0 // PAIR) * 16 * CH)
        order.close()
        raw.close()

        edges = sbuf(ctx, "edges", [P, NTL, 2], i32)
        dst_lane = sbuf(ctx, "dst_lane", [P, NTL], bf16)
        src_lane = sbuf(ctx, "src_lane", [P, NTL], bf16)
        src_block = sbuf(ctx, "src_block", [P, NTL], bf16)
        address1 = sbuf(ctx, "address1", [P, NT1], i32)
        tile_block2 = sbuf(ctx, "tile_block2", [1, NTB], i32)
        by_src = Rank("s", src_block[:, 0:NT1], NT1, address1[:, :], NT2, tile_block2, tile_block_dram[1])
        s_back = sem("s_back")
        split = ExitStack()
        tmp_e = sbuf(split, "tmp_e", [P, NTL], i32)
        with nc.Block() as block:
            @block.sync
            def _(sp):
                sp.dma_start(edges[:, :, :].rearrange("p t w -> p (t w)"),
                             edge_list.rearrange("(p t) w -> p (t w)", p=P)).then_inc(s_back, 16)

            @block.vector
            def _(dve):
                chain = vec_chain.on(dve)
                dve.wait_ge(s_back, 16)
                nc.vector.tensor_copy(dst_lane[:, :], edges[:, :, 1])
                chain(nc.vector.tensor_scalar(tmp_e[:, :], edges[:, :, 0], P - 1, None, ALU.bitwise_and))
                chain(nc.vector.tensor_copy(src_lane[:, :], tmp_e[:, :]))
                chain(nc.vector.tensor_scalar(tmp_e[:, :], edges[:, :, 0], 7, None, ALU.logical_shift_right))
                chain(nc.vector.tensor_copy(src_block[:, :], tmp_e[:, :]))
        split.close()

        def one_hot(to, lanes, n, width=P):
            return nc.vector.tensor_tensor(to, lane_row[:, 0:width].unsqueeze(1).to_broadcast([P, n, width]),
                                           lanes.unsqueeze(2).to_broadcast([P, n, width]), ALU.is_equal)

        def blocks_of(table, tiles_from, engine):
            return nc.values_load_multi_w_load_instructions(
                table[0:1, bass.ds(tiles_from, CH)], engines=[engine], min_val=0, max_val=BLOCKS - 1,
                skip_runtime_bounds_check_because="the table of tiles' blocks is clamped to the last block")[1]

        def aggregate(tag, table, with_degrees):
            s_idx, s_row = sem(f"s_idx{tag}"), [sem(f"s_row{tag}{b}") for b in range(2)]
            s_hot, s_mm, s_tick = sem(f"s_hot{tag}"), sem(f"s_mm{tag}"), sem(f"s_tick{tag}")
            own = ExitStack()
            idx = sbuf(own, f"idx{tag}", [P, 2, CH], i32)
            rows = sbuf(own, f"rows{tag}", [P, 2, CH, F])
            hot = sbuf(own, f"hot{tag}", [P, 2, CH, P])
            sum_banks = banks(own, f"sum_banks{tag}", 4)
            sum_ps = sum_banks[:, :, :].rearrange("p a (b f) -> p (a b) f", f=F)
            if with_degrees:
                hot_dl = sbuf(own, f"hot_dl{tag}", [P, 2, CH, P], bf16)
                hot_sl = sbuf(own, f"hot_sl{tag}", [P, 2, CH, P], bf16)
                hot_sb = sbuf(own, f"hot_sb{tag}", [P, 2, CH, P], bf16)
                deg_ps = banks(own, f"deg_ps{tag}", 2)
            turns = NT1 // PAIR
            with nc.Block() as block:
                @block.scalar
                def _(act):
                    for b in range(2):
                        nc.scalar.copy(idx[:, b, :], edges[:, b * CH:(b + 1) * CH, 0]).then_inc(s_idx, 1)
                    with act.Fori(0, turns) as i:
                        for b in range(2):
                            act.wait_ge(s_row[b], i * (16 * CH) + 16 * CH)
                            act.sem_inc(s_tick)
                            nc.scalar.copy(idx[:, b, :], edges[:, bass.ds(i * PAIR + (PAIR + b * CH), CH), 0]
                                           ).then_inc(s_idx, 1)

                @block.gpsimd
                def _(pool):
                    def gather(b):
                        for k in range(CH):
                            pool.indirect_dma_start(
                                out=rows[:, b, k, :], out_offset=None, in_=table,
                                in_offset=bass.IndirectOffsetOnAxis(ap=idx[:, b, k:k + 1], axis=0)
                            ).then_inc(s_row[b], 16)
                    for b in range(2):
                        pool.wait_ge(s_idx, b + 1)
                        gather(b)
                    with pool.Fori(0, turns) as i:
                        for b in range(2):
                            pool.wait_ge(s_idx, i * 2 + (b + 3))
                            pool.wait_ge(s_mm, i * 2 + (b + 3))
                            pool.sem_inc(s_tick)
                            gather(b)
                    for b in range(2):
                        pool.wait_ge(s_row[b], (turns + 1) * 16 * CH)

                @block.vector
                def _(dve):
                    if with_degrees:
                        dve.sem_inc(by_src.s_hist)
                    with dve.Fori(0, NT1 // QUAD) as i:
                        ranking = () if with_degrees else by_src.slots_of_block(i)
                        for q in range(4):
                            b = q % 2
                            at = bass.ds(i * QUAD + q * CH, CH)
                            dve.wait_ge(s_mm, i * 4 + (q + 1))
                            last = one_hot(hot[:, b, :, :], dst_lane[:, at], CH)
                            if with_degrees:
                                one_hot(hot_dl[:, b, :, :], dst_lane[:, at], CH)
                                one_hot(hot_sl[:, b, :, :], src_lane[:, at], CH)
                                last = one_hot(hot_sb[:, b, :, :], src_block[:, at], CH)
                            last.then_inc(s_hot, 1)
                            if with_degrees and q == 0:
                                by_src.count_block(dve, i)
                            if q < len(ranking):
                                ranking[q](dve)
                    chain = vec_chain.on(dve)
                    dve.wait_ge(s_mm, 2 * turns + 2)
                    chain(nc.vector.tensor_copy(sums, sum_ps[:, 0:BLOCKS, :]))
                    if with_degrees:
                        chain(nc.vector.tensor_copy(deg_dst[:, :], deg_ps[:, 0, 0:BLOCKS]))
                        chain(nc.vector.tensor_tensor(deg_sum[:, :], deg_dst[:, :], deg_ps[:, 1, 0:BLOCKS], ALU.add))
                    else:
                        by_src.addresses(chain)

                @block.tensor
                def _(pe):
                    pe.sem_inc(s_mm, 2)
                    for n in range(4):
                        nc.tensor.matmul(sum_banks[:, n, :], zeros[:, 0:P], zeros[:, 0:BANK], start=True, stop=True)
                    if with_degrees:
                        for n in range(2):
                            nc.tensor.matmul(deg_ps[:, n, 0:P], zeros[:, 0:P], zeros[:, 0:P], start=True, stop=True)
                    with pe.Fori(0, turns) as i:
                        for b in range(2):
                            at = blocks_of(tile_block, i * PAIR + b * CH, mybir.EngineType.PE)
                            pe.wait_ge(s_row[b], i * (16 * CH) + 16 * CH)
                            pe.wait_ge(s_hot, i * 2 + (b + 1))
                            pe.sem_inc(s_tick)
                            if with_degrees:
                                for k in range(CH):
                                    nc.tensor.matmul(deg_ps[:, 1, 0:P], hot_sl[:, b, k, :], hot_sb[:, b, k, :],
                                                     start=False, stop=True, skip_group_check=True)
                                for k in range(CH):
                                    nc.tensor.matmul(deg_ps[:, 0, bass.ds(at[k], 1)], hot_dl[:, b, k, :], ones_b[:, :],
                                                     start=False, stop=True, skip_group_check=True)
                            for k in range(CH):
                                to = sum_ps[:, bass.ds(at[k], 1), :].rearrange("p a f -> p (a f)")
                                last = nc.tensor.matmul(to, hot[:, b, k, :], rows[:, b, k, :], start=False, stop=True,
                                                        skip_group_check=True)
                            last.then_inc(s_mm, 1)

                if with_degrees:
                    @block.sync
                    def _(sp):
                        m = messages.rearrange("(p t) w -> p (t w)", p=P)
                        n = -(-NT2 * MROW // ZROW)
                        for j in range(n):
                            to = m[:, j * ZROW:min((j + 1) * ZROW, NT2 * MROW)]
                            sp.dma_start(to, zeros[:, 0:to.shape[1]]).then_inc(s_mfill, 16)
                        sp.wait_ge(s_mfill, 16 * n)
            own.close()

        s_mfill = sem("s_mfill")
        aggregate("a", x_table, True)
        by_src.place_blocks(HB + 1)

        s_cat, s_node, s_nt, s_ht = sem("s_cat"), sem("s_node"), sem("s_nt"), sem("s_ht")
        s_node_go = sem("s_node_go")
        own = ExitStack()
        cat = sbuf(own, "cat", [P, NBP, 2 * F])
        stage = sbuf(own, "stage", [P, P])
        stage_t = sbuf(own, "stage_t", [P, P])
        hidden = sbuf(own, "hidden", [HID1, GROUP * P])
        stage_ps = banks(own, "stage_ps")[:, 0, 0:P]
        hidden_ps = banks(own, "hidden_ps")[0:HID1, 0, :]
        out_ps = view(banks(own, "out_ps")[:, 0, :], GROUP, 2 * F)
        STEPS = 7
        with nc.Block() as block:
            @block.vector
            def _(dve):
                chain = vec_chain.on(dve)
                nc.vector.tensor_scalar(r_deg[:, :], deg_dst[:, :], 1.0, None, ALU.max)
                chain(nc.vector.memset(cat[:, BLOCKS:, 0:F], 0.0))
                nc.vector.tensor_copy(cat[:, :, F:2 * F], x_nodes[:, :, :])
                chain(nc.vector.reciprocal(r_deg[:, :], r_deg[:, :]))
                chain(nc.vector.tensor_tensor(cat[:, 0:BLOCKS, 0:F], sums,
                                              r_deg[:, :].unsqueeze(2).to_broadcast([P, BLOCKS, F]), ALU.mult))
                dve.sem_inc(s_cat)
                with dve.Fori(0, GROUPS) as g:
                    dve.wait_ge(s_node, g * STEPS + 6)
                    dve.sem_inc(s_nt)
                    nc.vector.tensor_copy(h_nodes[:, bass.ds(g * GROUP, GROUP), :], out_ps[:, :, :]
                                          ).then_inc(s_node, 1)
                dve.wait_ge(s_node, GROUPS * STEPS)

            @block.scalar
            def _(act):
                act.wait_ge(s_cat, 1)
                with act.Fori(0, GROUPS) as g:
                    act.wait_ge(s_node_go, g + 1)
                    act.sem_inc(s_nt)
                    nc.scalar.copy(stage[:, :], cat[:, bass.ds(g * GROUP, GROUP), :].rearrange("p b f -> p (b f)")
                                   ).then_inc(s_node, 1)
                    act.wait_ge(s_node, g * STEPS + 2)
                    act.sem_inc(s_nt)
                    nc.scalar.copy(stage_t[:, :], stage_ps[:, :]).then_inc(s_node, 1)
                    act.wait_ge(s_node, g * STEPS + 4)
                    act.sem_inc(s_nt)
                    nc.scalar.activation(hidden[:, :], hidden_ps[:, :], ACT.Relu, bias=b1c[:, 0:1]
                                         ).then_inc(s_node, 1)

            @block.tensor
            def _(pe):
                pe.sem_inc(s_node_go)
                with pe.Fori(0, GROUPS) as g:
                    pe.wait_ge(s_node, g * STEPS + 1)
                    pe.sem_inc(s_nt)
                    nc.tensor.transpose(stage_ps[:, :], stage[:, :], ident[:, :]).then_inc(s_node, 1)
                    pe.wait_ge(s_node, g * STEPS + 3)
                    pe.sem_inc(s_nt)
                    for j in range(GROUP):
                        last = nc.tensor.matmul(hidden_ps[:, j * P:(j + 1) * P], w1[:, j, :], stage_t[:, :],
                                                start=True, stop=True)
                    last.then_inc(s_node, 1)
                    pe.wait_ge(s_node, g * STEPS + 5)
                    pe.sem_inc(s_nt)
                    for j in range(GROUP):
                        last = nc.tensor.matmul(out_ps[:, j, :], hidden[:, j * P:(j + 1) * P], w2[:, :],
                                                start=True, stop=True)
                    last.then_inc(s_node, 1)
                    pe.wait_ge(s_node, g * STEPS + 7)
                    pe.sem_inc(s_node_go)

            @block.sync
            def _(sp):
                sp.wait_ge(s_node, GROUPS * STEPS)
                sp.dma_start(h_table.rearrange("(b l) f -> l b f", l=P), h_nodes[:, 0:BLOCKS, 0:F]).then_inc(s_ht, 16)
                sp.wait_ge(s_ht, 16)
        own.close()

        aggregate("b", h_table, False)

        own = ExitStack()
        t_sum = sbuf(own, "t_sum", [P, BLOCKS, F])
        t_sq = sbuf(own, "t_sq", [P, BLOCKS, F])
        t_mean = sbuf(own, "t_mean", [P, BLOCKS])
        t_var = sbuf(own, "t_var", [P, BLOCKS])
        t_deg = sbuf(own, "t_deg", [P, BLOCKS])
        rest = sbuf(own, "rest", [P, BLOCKS, ROW])
        s_sq, s_rt = sem("s_sq"), sem("s_rt")

        def wide(v):
            return v[:, :].unsqueeze(2).to_broadcast([P, BLOCKS, F])

        def layer_norm(dve, chain, to, turn):
            chain(nc.vector.tensor_reduce(t_mean[:, :], t_sum[:, :, :], AX, ALU.add))
            chain(nc.vector.tensor_scalar(t_mean[:, :], t_mean[:, :], 1.0 / F, None, ALU.mult))
            chain(nc.vector.tensor_tensor(t_sum[:, :, :], t_sum[:, :, :], wide(t_mean), ALU.subtract))
            chain(nc.vector.tensor_tensor(t_sq[:, :, :], t_sum[:, :, :], t_sum[:, :, :], ALU.mult))
            chain(nc.vector.tensor_reduce(t_var[:, :], t_sq[:, :, :], AX, ALU.add))
            chain(nc.vector.tensor_scalar(t_var[:, :], t_var[:, :], 1.0 / F, LN_EPS, ALU.mult, ALU.add))
            dve.sem_inc(s_sq)
            dve.wait_ge(s_rt, turn)
            chain(nc.vector.reciprocal(t_var[:, :], t_var[:, :]))
            chain(nc.vector.tensor_tensor(to, t_sum[:, :, :], wide(t_var), ALU.mult))

        s_y = sem("s_y")
        with nc.Block() as block:
            @block.vector
            def _(dve):
                chain = vec_chain.on(dve)
                chain(nc.vector.tensor_scalar(t_deg[:, :], deg_sum[:, :], 1e-5, None, ALU.max))
                chain(nc.vector.tensor_tensor(t_sum[:, :, :], sums, wide(r_deg), ALU.mult))
                chain(nc.vector.tensor_tensor(t_sum[:, :, :], t_sum[:, :, :], h_nodes[:, 0:BLOCKS, F:2 * F], ALU.add))
                chain(nc.vector.tensor_tensor(t_sum[:, :, :], t_sum[:, :, :],
                                              b2r[:, :].unsqueeze(1).to_broadcast([P, BLOCKS, F]), ALU.add))
                chain(nc.vector.tensor_tensor(t_sum[:, :, :], t_sum[:, :, :], x_nodes[:, 0:BLOCKS, :], ALU.add))
                layer_norm(dve, chain, y_nodes[:, 0:BLOCKS, 0:F], 2)
                chain(nc.vector.reciprocal(y_nodes[:, 0:BLOCKS, F], t_deg[:, :]))
                chain(nc.vector.tensor_copy(y_parts[:, :, 0, :], y_nodes[:, 0:BLOCKS, :]))
                chain(nc.vector.tensor_tensor(rest[:, :, :], y_nodes[:, 0:BLOCKS, :], y_parts[:, :, 0, :], ALU.subtract))
                chain(nc.vector.tensor_copy(y_parts[:, :, 1, :], rest[:, :, :]))
                chain(nc.vector.tensor_tensor(y_parts[:, :, 2, :], rest[:, :, :], y_parts[:, :, 1, :], ALU.subtract))
                dve.sem_inc(s_y)

            @block.scalar
            def _(act):
                act.wait_ge(s_sq, 1)
                nc.scalar.sqrt(t_deg[:, :], t_deg[:, :]).then_inc(s_rt, 1)
                nc.scalar.sqrt(t_var[:, :], t_var[:, :]).then_inc(s_rt, 1)

            @block.sync
            def _(sp):
                sp.wait_ge(s_y, 1)
                sp.dma_start(y_table.rearrange("(b l) f -> l b f", l=P), y_nodes[:, 0:BLOCKS, :]).then_inc(s_y, 16)
                sp.wait_ge(s_y, 17)
        own.close()

        s_idx, s_adr, s_msg = sem("s_idx3"), sem("s_adr3"), sem("s_msg3")
        s_row = [sem(f"s_row3{b}") for b in range(2)]
        s_put = [sem(f"s_put3{b}") for b in range(2)]
        s_hot, s_hott, s_hotc, s_ownr = sem("s_hot3"), sem("s_hott"), sem("s_hotc"), sem("s_own3")
        s_xc, s_xt, s_xtc, s_hid, s_hidr, s_map = (sem(n) for n in ("s_xc", "s_xt", "s_xtc", "s_hid", "s_hidr", "s_map"))
        s_free = sem("s_free")
        s_msg2 = sem("s_msg2")
        s_mapu, s_mm, s_add, s_tick, s_d = (sem(n) for n in ("s_mapu", "s_mm3", "s_add3", "s_tick3", "s_d3"))
        own = ExitStack()
        idx = sbuf(own, "idx3", [P, 2, CH], i32)
        adr = sbuf(own, "adr3", [P, 2, CH], i32)
        rows = sbuf(own, "rows3", [P, 2, CH, ROW])
        hot = sbuf(own, "hot3", [P, 2, CH, P], bf16)
        hot_t = sbuf(own, "hot_t", [P, CH, P], bf16)
        xx = sbuf(own, "xx", [P, 2, CH, 2, F])
        inv = sbuf(own, "inv", [P, 2, CH, 2])
        xx_t = sbuf(own, "xx_t", [P, 2, P])
        hid = sbuf(own, "hid", [P, CH, P])
        v = sbuf(own, "v", [P, CH, 2, F])
        t = sbuf(own, "t", [P, CH, 2, F])
        t2 = sbuf(own, "t2", [P, CH, 2, F])
        w = sbuf(own, "w", [P, CH, 2, F])
        n2 = sbuf(own, "n2", [P, CH, 2])
        d = sbuf(own, "d", [P, CH, 2])
        msg = sbuf(own, "msg", [P, 2, CH, 2, MROW])
        msg_b = msg[:, :, :, :, :].rearrange("p b k e m -> p (b k e m)").bitcast(bf16).rearrange(
            "p (b k e m) -> p b k e m", b=2, k=CH, e=2)
        hot_ps = banks(own, "hot_ps")[:, 0, :].bitcast(bf16).rearrange("p (k l) -> p k l", l=P)
        own_ps = view(banks(own, "own_ps")[:, 0, :], CH, ROW)
        xx_ps = view(banks(own, "xx_ps")[:, 0, :], 2, P)
        hid_ps = banks(own, "hid_ps", 2)[:, :, :].rearrange("p a (k l) -> p (a k) l", l=P)
        map_ps = view(banks(own, "map_ps")[:, 0, :], CH, 2 * F)
        sum_ps = view(banks(own, "sum_ps3")[:, 0, :], CH, F)
        turns = NT1 // PAIR
        DSTEPS = 18
        with nc.Block() as block:
            @block.gpsimd
            def _(pool):
                def gather(b):
                    for k in range(CH):
                        pool.indirect_dma_start(
                            out=rows[:, b, k, :], out_offset=None, in_=y_table,
                            in_offset=bass.IndirectOffsetOnAxis(ap=idx[:, b, k:k + 1], axis=0)
                        ).then_inc(s_row[b], 16)
                pool.sem_inc(s_free, 2)
                for b in range(2):
                    pool.wait_ge(s_idx, b + 1)
                    gather(b)
                with pool.Fori(0, turns) as i:
                    for b in range(2):
                        pool.wait_ge(s_msg, i * 2 + (b + 1))
                        pool.wait_ge(s_adr, i * 2 + (b + 1))
                        pool.wait_ge(s_xc, i * 2 + (b + 1))
                        pool.wait_ge(s_idx, i * 2 + (b + 3))
                        pool.sem_inc(s_tick)
                        for k in range(CH):
                            pool.indirect_dma_start(
                                out=messages, out_offset=bass.IndirectOffsetOnAxis(ap=adr[:, b, k:k + 1], axis=0),
                                in_=msg[:, b, k, 0, :], in_offset=None).then_inc(s_put[b], 16)
                        gather(b)
                        pool.wait_ge(s_put[b], i * (16 * CH) + 16 * CH)
                        pool.sem_inc(s_free)
                for b in range(2):
                    pool.wait_ge(s_row[b], (turns + 1) * 16 * CH)

            @block.scalar
            def _(act):
                def copy_hot(c):
                    act.wait_ge(s_hott, c + 1)
                    act.sem_inc(s_tick)
                    nc.scalar.copy(hot_t[:, :, :], hot_ps).then_inc(s_hotc, 1)
                for b in range(2):
                    nc.scalar.copy(idx[:, b, :], edges[:, b * CH:(b + 1) * CH, 0]).then_inc(s_idx, 1)
                def ends(c, b, row_count, idx_from):
                    copy_hot(c)
                    act.wait_ge(s_row[b], row_count)
                    act.wait_ge(s_ownr, c + 1)
                    act.wait_ge(s_msg2, c + 1)
                    act.sem_inc(s_tick)
                    nc.scalar.copy(xx[:, b, :, 0, :], rows[:, b, :, 0:F])
                    nc.scalar.copy(xx[:, b, :, 1, :], own_ps[:, :, 0:F])
                    nc.scalar.copy(inv[:, b, :, 1], rows[:, b, :, F])
                    nc.scalar.copy(inv[:, b, :, 0], own_ps[:, :, F]).then_inc(s_xc, 1)
                    if idx_from is not None:
                        nc.scalar.copy(idx[:, b, :], edges[:, bass.ds(idx_from, CH), 0]).then_inc(s_idx, 1)
                    act.wait_ge(s_xt, c + 1)
                    act.sem_inc(s_tick)
                    nc.scalar.copy(xx_t[:, :, :], xx_ps[:, :, :]).then_inc(s_xtc, 1)
                    act.wait_ge(s_hid, c + 1)
                    act.sem_inc(s_tick)
                    for half in range(2):
                        last = nc.scalar.activation(hid[:, half * 4:half * 4 + 4, :],
                                                    hid_ps[:, half * 4:half * 4 + 4, :], ACT.Relu,
                                                    bias=v1c[:, 0:1])
                    last.then_inc(s_hidr, 1)
                ends(0, 0, 16 * CH, PAIR)
                with act.Fori(0, turns) as i:
                    for b in range(2):
                        c = i * 2 + b
                        act.wait_ge(s_free, c + 1)
                        act.sem_inc(s_tick)
                        nc.scalar.copy(msg_b[:, b, :, 0, PARTS * F], src_lane[:, bass.ds(i * PAIR + b * CH, CH)])
                        nc.scalar.copy(adr[:, b, :], address1[:, bass.ds(i * PAIR + b * CH, CH)]).then_inc(s_adr, 1)
                        ends(c + 1, 1 - b, i * (16 * CH) + 16 * CH * (b + 1), i * PAIR + (b + 3) * CH)

            @block.tensor
            def _(pe):
                def own_rows(c, b, at):
                    blocks = blocks_of(tile_block, at, mybir.EngineType.PE)
                    pe.wait_ge(s_hot, c + 1)
                    pe.sem_inc(s_tick)
                    for k in range(CH):
                        last = nc.tensor.transpose(hot_ps[:, k, :], hot[:, b, k, :], ident_b[:, :])
                    last.then_inc(s_hott, 1)
                    pe.wait_ge(s_hotc, c + 1)
                    pe.sem_inc(s_tick)
                    for k in range(CH):
                        for j in range(PARTS):
                            last = nc.tensor.matmul(
                                own_ps[:, k, :], hot_t[:, k, :],
                                y_parts[:, bass.ds(blocks[k], 1), j, :].rearrange("p a f -> p (a f)"),
                                start=(j == 0), stop=(j == PARTS - 1))
                    last.then_inc(s_ownr, 1)
                def hiddens(c, b):
                    pe.wait_ge(s_xc, c + 1)
                    pe.sem_inc(s_tick)
                    for g in range(2):
                        last = nc.tensor.transpose(
                            xx_ps[:, g, :], xx[:, b, 4 * g:4 * g + 4, :, :].rearrange("p k e f -> p (k e f)"),
                            ident[:, :])
                    last.then_inc(s_xt, 1)
                    pe.wait_ge(s_xtc, c + 1)
                    pe.sem_inc(s_tick)
                    for k in range(CH):
                        last = nc.tensor.matmul(hid_ps[:, k, :], v1[:, k % GROUP, :], xx_t[:, k // GROUP, :],
                                                start=True, stop=True)
                    last.then_inc(s_hid, 1)

                def maps(c):
                    pe.wait_ge(s_hidr, c + 1)
                    pe.wait_ge(s_mapu, c + 1)
                    pe.sem_inc(s_tick)
                    for k in range(CH):
                        last = nc.tensor.matmul(map_ps[:, k, :], hid[:, k, :], v2[:, :], start=True, stop=True)
                    last.then_inc(s_map, 1)
                own_rows(0, 0, 0)
                hiddens(0, 0)
                maps(0)
                with pe.Fori(0, turns) as i:
                    for b in range(2):
                        c = i * 2 + b
                        own_rows(c + 1, 1 - b, i * PAIR + (b + 1) * CH)
                        hiddens(c + 1, 1 - b)
                        pe.wait_ge(s_msg2, c + 2)
                        pe.wait_ge(s_add, c + 1)
                        pe.sem_inc(s_tick)
                        for k in range(CH):
                            for j in range(PARTS):
                                last = nc.tensor.matmul(sum_ps[:, k, :], hot[:, b, k, :],
                                                        msg_b[:, b, k, 1, j * F:(j + 1) * F],
                                                        start=(j == 0), stop=(j == PARTS - 1))
                        last.then_inc(s_mm, 1)
                        maps(c + 1)

            @block.vector
            def _(dve):
                def pairs(x):
                    return x.unsqueeze(3).to_broadcast([P, CH, 2, F])

                dve.sem_inc(s_mapu)
                dve.sem_inc(s_msg2)
                nc.vector.memset(msg[:, :, :, :, :], 0.0)
                nc.vector.memset(acc[:, :, :, :], 0.0).then_inc(s_add, 1)
                for b in range(2):
                    one_hot(hot[:, b, :, :], dst_lane[:, b * CH:(b + 1) * CH], CH).then_inc(s_hot, 1)
                steps = Chain(dve, s_d)
                with dve.Fori(0, turns) as i:
                    steps.turn(i, 2 * DSTEPS)
                    for b in range(2):
                        c = i * 2 + b
                        x_both = xx[:, b, :, :, :]
                        dve.wait_ge(s_map, c + 1)
                        steps(nc.vector.tensor_tensor(
                            v[:, :, :, :].rearrange("p k e f -> p k (e f)"), map_ps[:, :, :],
                            v2r[:, :].unsqueeze(1).to_broadcast([P, CH, 2 * F]), ALU.add))
                        dve.sem_inc(s_mapu)
                        nc.vector.tensor_tensor(t[:, :, :, :], v[:, :, :, :], v[:, :, :, :], ALU.mult)
                        steps(nc.vector.tensor_tensor(t2[:, :, :, :], v[:, :, :, :], x_both, ALU.mult))
                        nc.vector.tensor_reduce(d[:, :, :], t2[:, :, :, :], AX, ALU.add)
                        steps(nc.vector.tensor_reduce(n2[:, :, :], t[:, :, :, :], AX, ALU.add))
                        steps(nc.vector.tensor_scalar(n2[:, :, :], n2[:, :, :], NORM_EPS2, 0.5, ALU.max, ALU.mult))
                        steps(nc.vector.reciprocal(n2[:, :, :], n2[:, :, :]))
                        steps(nc.vector.tensor_tensor(d[:, :, :], d[:, :, :], n2[:, :, :], ALU.mult))
                        steps(nc.vector.tensor_tensor(t[:, :, :, :], v[:, :, :, :], pairs(d[:, :, :]), ALU.mult))
                        nc.vector.tensor_tensor(w[:, :, 0, :], x_both[:, :, 1, :], t[:, :, 1, :], ALU.subtract)
                        steps(nc.vector.tensor_tensor(w[:, :, 1, :], x_both[:, :, 0, :], t[:, :, 0, :], ALU.subtract))
                        steps(nc.vector.tensor_tensor(t2[:, :, :, :], v[:, :, :, :], w[:, :, :, :], ALU.mult))
                        steps(nc.vector.tensor_reduce(d[:, :, :], t2[:, :, :, :], AX, ALU.add))
                        steps(nc.vector.tensor_tensor(d[:, :, :], d[:, :, :], n2[:, :, :], ALU.mult))
                        steps(nc.vector.tensor_tensor(t[:, :, :, :], v[:, :, :, :], pairs(d[:, :, :]), ALU.mult))
                        steps(nc.vector.tensor_tensor(w[:, :, :, :], w[:, :, :, :], t[:, :, :, :], ALU.subtract))
                        steps(nc.vector.tensor_tensor(t[:, :, :, :], w[:, :, :, :], pairs(inv[:, b, :, :]), ALU.mult))
                        to = [msg_b[:, b, :, :, j * F:(j + 1) * F] for j in range(PARTS)]
                        dve.wait_ge(s_free, c + 1)
                        steps(nc.vector.tensor_copy(to[0], t[:, :, :, :]))
                        steps(nc.vector.tensor_tensor(t2[:, :, :, :], t[:, :, :, :], to[0], ALU.subtract))
                        steps(nc.vector.tensor_copy(to[1], t2[:, :, :, :]))
                        steps(nc.vector.tensor_tensor(to[2], t2[:, :, :, :], to[1], ALU.subtract))
                        dve.sem_inc(s_msg)
                        dve.sem_inc(s_msg2)
                        at = blocks_of(tile_block, i * PAIR + b * CH, mybir.EngineType.DVE)
                        dve.wait_ge(s_mm, c + 1)
                        dve.wait_ge(s_add, c + 1)
                        for k in range(CH):
                            to = acc[:, k, bass.ds(at[k], 1), 0:F].rearrange("p a f -> p (a f)")
                            last = nc.vector.tensor_tensor(to, to, sum_ps[:, k, :], ALU.add)
                        last.then_inc(s_add, 1)
                        one_hot(hot[:, b, :, :], dst_lane[:, bass.ds(i * PAIR + (b + 2) * CH, CH)], CH
                                ).then_inc(s_hot, 1)
                chain = vec_chain.on(dve)
                dve.wait_ge(s_add, 2 * turns + 1)
                for half in (4, 2, 1):
                    chain(nc.vector.tensor_tensor(acc[:, 0:half, :, 0:F], acc[:, 0:half, :, 0:F],
                                                  acc[:, half:2 * half, :, 0:F], ALU.add))
        own.close()

        own = ExitStack()
        DEEP = 4
        s_in = [sem(f"s_in{q}") for q in range(DEEP)]
        s_hot, s_mm, s_tick = sem("s_hot4"), sem("s_mm4"), sem("s_tick4")
        got = sbuf(own, "got", [P, DEEP, CH, MROW])
        got_b = got[:, :, :, :].rearrange("p q k m -> p (q k m)").bitcast(bf16).rearrange(
            "p (q k m) -> p q k m", q=DEEP, k=CH)
        hot = sbuf(own, "hot4", [P, DEEP, CH, P], bf16)
        sum_banks = banks(own, "sum_banks4", 4)
        sum_ps = sum_banks[:, :, :].rearrange("p a (b f) -> p (a b) f", f=F)
        m_rows = messages.rearrange("(p t) w -> p t w", p=P)
        turns4 = NT2 // (DEEP * CH)
        with nc.Block() as block:
            @block.sync
            def _(sp):
                with sp.Fori(0, turns4) as i:
                    for q in range(DEEP):
                        sp.wait_ge(s_mm, i * DEEP + (q + 1))
                        sp.sem_inc(s_tick)
                        sp.dma_start(got[:, q, :, :], m_rows[:, bass.ds(i * (DEEP * CH) + q * CH, CH), :]
                                     ).then_inc(s_in[q], 16)

            @block.vector
            def _(dve):
                with dve.Fori(0, turns4) as i:
                    for q in range(DEEP):
                        dve.wait_ge(s_in[q], i * 16 + 16)
                        dve.wait_ge(s_mm, i * DEEP + (q + 1))
                        dve.sem_inc(s_tick)
                        one_hot(hot[:, q, :, :], got_b[:, q, :, PARTS * F], CH).then_inc(s_hot, 1)
                chain = vec_chain.on(dve)
                dve.wait_ge(s_mm, NT2 // CH + DEEP)
                chain(nc.vector.tensor_tensor(acc[:, 0, :, 0:F], acc[:, 0, :, 0:F], sum_ps[:, 0:BLOCKS, :], ALU.add))

            @block.tensor
            def _(pe):
                pe.sem_inc(s_mm, DEEP)
                for n in range(4):
                    nc.tensor.matmul(sum_banks[:, n, :], zeros[:, 0:P], zeros[:, 0:BANK], start=True, stop=True)
                with pe.Fori(0, turns4) as i:
                    for q in range(DEEP):
                        at = blocks_of(tile_block2, i * (DEEP * CH) + q * CH, mybir.EngineType.PE)
                        pe.wait_ge(s_in[q], i * 16 + 16)
                        pe.wait_ge(s_hot, i * DEEP + (q + 1))
                        pe.sem_inc(s_tick)
                        for k in range(CH):
                            to = sum_ps[:, bass.ds(at[k], 1), :].rearrange("p a f -> p (a f)")
                            for j in range(PARTS):
                                last = nc.tensor.matmul(to, hot[:, q, k, :], got_b[:, q, k, j * F:(j + 1) * F],
                                                        start=False, stop=True, skip_group_check=True)
                        last.then_inc(s_mm, 1)
        own.close()

        own = ExitStack()
        t_sum = sbuf(own, "t_sum5", [P, BLOCKS, F])
        t_sq = sbuf(own, "t_sq5", [P, BLOCKS, F])
        t_mean = sbuf(own, "t_mean5", [P, BLOCKS])
        t_var = sbuf(own, "t_var5", [P, BLOCKS])
        s_fin = sem("s_fin")
        y = y_nodes[:, 0:BLOCKS, 0:F]
        with nc.Block() as block:
            @block.vector
            def _(dve):
                chain = vec_chain.on(dve)
                chain(nc.vector.tensor_tensor(t_sum[:, :, :], acc[:, 0, :, 0:F],
                                              y_nodes[:, 0:BLOCKS, F:ROW].to_broadcast([P, BLOCKS, F]), ALU.mult))
                chain(nc.vector.tensor_tensor(t_sum[:, :, :], t_sum[:, :, :], y, ALU.add))
                chain(nc.vector.tensor_scalar(t_sum[:, :, :], t_sum[:, :, :], 0.0, None, ALU.max))
                chain(nc.vector.tensor_tensor(t_sum[:, :, :], t_sum[:, :, :], y, ALU.add))
                layer_norm(dve, chain, t_sq[:, :, :], 3)
                dve.sem_inc(s_fin)

            @block.scalar
            def _(act):
                act.wait_ge(s_sq, 2)
                nc.scalar.sqrt(t_var[:, :], t_var[:, :]).then_inc(s_rt, 1)

            @block.sync
            def _(sp):
                sp.wait_ge(s_fin, 1)
                whole = NODES // P
                sp.dma_start(out[0:whole * P, :].rearrange("(b l) f -> l b f", l=P), t_sq[:, 0:whole, :]
                             ).then_inc(s_fin, 16)
                sp.dma_start(out[whole * P:NODES, :], t_sq[0:NODES - whole * P, whole, :]).then_inc(s_fin, 16)
                sp.wait_ge(s_fin, 33)
        own.close()


_INS = ['x', 'src', 'dst', 'L0_gnn_W1_l', 'L0_gnn_b1', 'L0_gnn_W1_r', 'L0_gnn_W2_l', 'L0_gnn_b2', 'L0_gnn_W2_r',
        'L1_gnn_W1', 'L1_gnn_b1', 'L1_gnn_W2', 'L1_gnn_b2']
_OUTS = [((NODES, F), 'float32')]


def kernel(**inputs):
    import numpy as _np
    import concourse.bacc as _bacc
    from concourse import mybir as _mybir
    from concourse.bass_utils import run_bass_kernel_spmd as _run

    nc = _bacc.Bacc("TRN2", target_bir_lowering=False, num_devices=1)
    arrays, args = {}, []
    for name in _INS:
        a = _np.ascontiguousarray(inputs[name])
        arrays[f"in_{name}_dram"] = a
        args.append(nc.dram_tensor(f"in_{name}_dram", a.shape, _mybir.dt.from_np(a.dtype), kind="ExternalInput").ap())
    for i, (shape, dtype) in enumerate(_OUTS):
        dt = _mybir.dt.from_np(_np.dtype(dtype))
        args.append(nc.dram_tensor(f"out_{i}_dram", shape, dt, kind="ExternalOutput").ap())
    gnn(nc, *args)
    r = _run(nc, [arrays], core_ids=[0])
    got = tuple(r.results[0][f"out_{i}_dram"] for i in range(len(_OUTS)))
    return got[0]
```

```python
import concourse.bass as bass
from concourse import mybir
from contextlib import ExitStack

fp32 = mybir.dt.float32
bf16 = mybir.dt.bfloat16
i32 = mybir.dt.int32
ALU = mybir.AluOpType
ACT = mybir.ActivationFunctionType
AX = mybir.AxisListType.X


def up(n, m):
    return -(-n // m) * m


P = 128
F = 16
NODES = 12500
EDGES = 412500
BLOCKS = -(-NODES // P)
PAD_NODE = BLOCKS * P - 1
GROUP = 4
TRACKS = 2
GROUPS = up(-(-BLOCKS // GROUP), TRACKS)
NBP = GROUPS * GROUP
HID1, HID2 = 32, 64
CH = 8
PAIR = 2 * CH
QUAD = 4 * CH

NT0 = up(-(-EDGES // P), PAIR)
NT1 = up((EDGES + BLOCKS * (P - 1)) // P, QUAD)
NTL = NT1 + QUAD
NT2 = up((NT1 * P + BLOCKS * (P - 1)) // P, QUAD)
NTB = up(max(NTL, NT2), P)
HB = NT1 // QUAD
assert BLOCKS <= HB <= P
ROW = F + 1
PARTS = 3
MROW = (PARTS * F + 2) // 2
NO_LANE = 255
ROWS = -(-NTL // P)
assert NTL * P >= NT0 * P + BLOCKS * (P - 1) and ROWS * (3 * P + P // 2) <= CH * BLOCKS * F
BANK = 512
FILLS = 8
LN_EPS = 1e-5
NORM_EPS2 = 1e-24


class Chain:

    def __init__(self, eng, sem):
        self.eng, self.sem, self.n, self.base = eng, sem, 0, None

    def __call__(self, ins):
        ins.then_inc(self.sem, 1)
        self.n += 1
        self.eng.wait_ge(self.sem, self.n if self.base is None else self.base + self.n)

    def on(self, eng):
        self.eng = eng
        return self

    def turn(self, i, per_turn):
        self.base, self.n = i * per_turn, 0


def gnn(nc, x, src, dst, W1l, b1, W1r, W2l, b2, W2r, V1, c1, V2, c2, out):
    ctx = ExitStack()
    sems = {}

    def sem(name):
        sems[name] = ctx.enter_context(nc.semaphore(name))
        return sems[name]

    def sbuf(stack, name, shape, dt=fp32):
        return stack.enter_context(nc.sbuf_tensor(name, shape, dt))

    def banks(stack, name, n=1):
        return stack.enter_context(nc.psum_tensor(name, [P, n, BANK], fp32))

    def view(bank, n, m):
        return bank[:, 0:n * m].rearrange("p (n m) -> p n m", n=n)

    x_table = nc.dram_tensor("x_table", [BLOCKS * P, F], fp32).ap()
    h_table = nc.dram_tensor("h_table", [BLOCKS * P, F], fp32).ap()
    y_table = nc.dram_tensor("y_table", [BLOCKS * P, ROW], fp32).ap()
    given_list = nc.dram_tensor("given_list", [NT0 + 2, P], i32).ap()
    slot_list = nc.dram_tensor("slot_list", [P * NTL, 1], i32).ap()
    messages = nc.dram_tensor("messages", [P * NT2, MROW], fp32).ap()
    tile_block_dram = [nc.dram_tensor(f"tile_block_dram{n}", [NTB], i32).ap() for n in range(2)]

    with ctx:
        lane_row = sbuf(ctx, "lane_row", [P, P])
        part = sbuf(ctx, "part", [P, 1])
        ident = sbuf(ctx, "ident", [P, P])
        ident_b = sbuf(ctx, "ident_b", [P, P], bf16)
        ones_b = sbuf(ctx, "ones_b", [P, 1], bf16)
        before = sbuf(ctx, "before", [P, P])
        ones = sbuf(ctx, "ones", [P, P])
        zeros = sbuf(ctx, "zeros", [P, BANK])
        x_nodes = sbuf(ctx, "x_nodes", [P, NBP, F])
        h_nodes = sbuf(ctx, "h_nodes", [P, NBP, 2 * F])
        y_nodes = sbuf(ctx, "y_nodes", [P, NBP, ROW])
        y_parts = sbuf(ctx, "y_parts", [P, BLOCKS, PARTS, ROW], bf16)
        r_deg = sbuf(ctx, "r_deg", [P, BLOCKS])
        deg_sum = sbuf(ctx, "deg_sum", [P, BLOCKS])
        deg_dst = sbuf(ctx, "deg_dst", [P, BLOCKS])
        acc = sbuf(ctx, "acc", [P, CH, BLOCKS, F])
        hist = sbuf(ctx, "hist", [P, HB])
        first = sbuf(ctx, "first", [P, HB])
        tiles = sbuf(ctx, "tiles", [P, HB])
        ends = sbuf(ctx, "ends", [P, HB])
        total = sbuf(ctx, "total", [P, HB])
        tile_block = sbuf(ctx, "tile_block", [1, NTB], i32)
        tile_block2 = sbuf(ctx, "tile_block2", [1, NTB], i32)
        src_node = sbuf(ctx, "src_node", [P, NTL], i32)
        src_lane = sbuf(ctx, "src_lane", [P, NTL], bf16)
        src_block = sbuf(ctx, "src_block", [P, NTL], bf16)
        dst_lane = sbuf(ctx, "dst_lane", [P, NTL], bf16)
        address = sbuf(ctx, "address", [P, NT1], i32)
        shift = sbuf(ctx, "shift", [P, P])
        order_flag = sbuf(ctx, "order_flag", [P, 1], i32)
        w1 = sbuf(ctx, "w1", [P, GROUP, HID1])
        w2 = sbuf(ctx, "w2", [HID1, 2 * F])
        b1c = sbuf(ctx, "b1c", [HID1, 1])
        b2r = sbuf(ctx, "b2r", [P, F])
        v1 = sbuf(ctx, "v1", [P, GROUP, P])
        v1c = sbuf(ctx, "v1c", [P, 1])
        v2 = sbuf(ctx, "v2", [P, 2 * F])
        v2r = sbuf(ctx, "v2r", [P, 2 * F])

        s_vec = sem("s_vec")
        vec_chain = Chain(None, s_vec)

        s_const, s_fill, s_load, s_w = sem("s_const"), sem("s_fill"), sem("s_load"), sem("s_w")
        raw = ExitStack()
        src_raw = sbuf(raw, "src_raw", [P, NT0], i32)
        dst_raw = sbuf(raw, "dst_raw", [P, NT0], i32)
        setup = ExitStack()
        list_fill = sbuf(setup, "list_fill", [P, NTL // FILLS], i32)
        with nc.Block() as block:
            @block.gpsimd
            def _(pool):
                nc.gpsimd.iota(lane_row[:, :], [[1, P]], base=0, channel_multiplier=0,
                               allow_small_or_imprecise_dtypes=True)
                nc.gpsimd.iota(part[:, :], [[1, 1]], base=0, channel_multiplier=1,
                               allow_small_or_imprecise_dtypes=True).then_inc(s_const, 1)

            @block.vector
            def _(dve):
                chain = vec_chain.on(dve)
                nc.vector.memset(zeros[:, :], 0.0)
                nc.vector.memset(ones[:, :], 1.0)
                nc.vector.memset(v2[:, :], 0.0)
                nc.vector.memset(w1[:, :, :], 0.0)
                nc.vector.memset(v1[:, :, :], 0.0)
                nc.vector.memset(y_nodes[:, :, :], 0.0)
                nc.vector.memset(x_nodes[:, :, :], 0.0)
                nc.vector.memset(src_raw[:, :], PAD_NODE)
                nc.vector.memset(dst_raw[:, :], PAD_NODE)
                nc.vector.memset(hist[:, :], 0.0)
                chain(nc.vector.memset(list_fill[:, :], -1))
                dve.sem_inc(s_fill)
                dve.wait_ge(s_const, 1)
                nc.vector.memset(ones_b[:, :], 1.0)
                nc.vector.tensor_scalar(shift[:, :], lane_row[:, :], part[:, 0:1], -1.0, ALU.subtract, ALU.is_equal)
                nc.vector.tensor_scalar(ident_b[:, :], lane_row[:, :], part[:, 0:1], None, ALU.is_equal)
                nc.vector.tensor_scalar(ident[:, :], lane_row[:, :], part[:, 0:1], None, ALU.is_equal)
                chain(nc.vector.tensor_scalar(before[:, :], lane_row[:, :], part[:, 0:1], None, ALU.is_gt))

            @block.sync
            def _(sp):
                sp.wait_ge(s_fill, 1)
                full = EDGES // NT0
                for raw_sb, given in ((src_raw, src), (dst_raw, dst)):
                    sp.dma_start(raw_sb[0:full, :], given[0:full * NT0].rearrange("(p t) -> p t", p=full)
                                 ).then_inc(s_load, 16)
                    sp.dma_start(raw_sb[full:full + 1, 0:EDGES - full * NT0],
                                 given[full * NT0:EDGES].rearrange("(p t) -> p t", p=1)).then_inc(s_load, 16)
                lists = slot_list.rearrange("(p t) w -> p (t w)", p=P)
                for j in range(FILLS):
                    sp.dma_start(lists[:, j * (NTL // FILLS):(j + 1) * (NTL // FILLS)], list_fill[:, :]
                                 ).then_inc(s_load, 16)
                sp.dma_start(given_list[NT0:NT0 + 2, :], list_fill[0:2, 0:P]).then_inc(s_load, 16)
                sp.dma_start(x_table[0:NODES, :], x).then_inc(s_load, 16)
                sp.dma_start(x_table[NODES:, :], zeros[0:BLOCKS * P - NODES, 0:F]).then_inc(s_load, 16)
                whole = NODES // P
                sp.dma_start(x_nodes[:, 0:whole, :], x[0:whole * P, :].rearrange("(b l) f -> l b f", l=P)
                             ).then_inc(s_load, 16)
                sp.dma_start(x_nodes[0:NODES - whole * P, whole, :], x[whole * P:NODES, :]).then_inc(s_load, 16)
                sp.wait_ge(s_load, 16 * (FILLS + 9))

            @block.scalar
            def _(act):
                act.wait_ge(s_fill, 1)
                v1t = V1.rearrange("h k -> k h")
                loads = [(w2[:, 0:F], W2l), (w2[:, F:2 * F], W2r), (b1c[:, :], b1.rearrange("(h o) -> h o", o=1)),
                         (b2r[:, :], b2.partition_broadcast(P)),
                         (v1c[0:HID2, :], c1.rearrange("(h o) -> h o", o=1)),
                         (v1c[HID2:P, :], c1.rearrange("(h o) -> h o", o=1)),
                         (v2[0:HID2, 0:F], V2.rearrange("d h -> h d")),
                         (v2[HID2:P, F:2 * F], V2.rearrange("d h -> h d")),
                         (v2r[:, 0:F], c2.partition_broadcast(P)), (v2r[:, F:2 * F], c2.partition_broadcast(P))]
                for g in range(GROUP):
                    r = 2 * F * g
                    loads += [(w1[r:r + F, g, :], W1l), (w1[r + F:r + 2 * F, g, :], W1r),
                              (v1[r:r + 2 * F, g, 0:HID2], v1t),
                              (v1[r:r + F, g, HID2:P], v1t[F:2 * F, :]), (v1[r + F:r + 2 * F, g, HID2:P], v1t[0:F, :])]
                with nc.allow_non_contiguous_dma("small weights, once"):
                    for to, of in loads:
                        act.dma_start(to, of).then_inc(s_w, 16)
                act.wait_ge(s_w, 16 * len(loads))
        setup.close()

        acc_flat = acc[:, :, :, :].rearrange("p k b f -> p (k b f)")
        count = acc_flat[:, 0:NT1]
        slot = acc_flat[:, NT1:2 * NT1]
        mask = acc_flat[:, 2 * NT1:2 * NT1 + NT1 // 2].bitcast(bf16)
        sums = acc_flat[:, 3 * NT1:3 * NT1 + BLOCKS * F].rearrange("p (b f) -> p b f", f=F)

        class Rank:

            def __init__(self, tag, block_of, n, address, pitch, table, table_dram):
                self.tag, self.block_of, self.n, self.address, self.pitch = tag, block_of, n, address, pitch
                self.table, self.table_dram = table, table_dram
                self.s_rtick = sem(f"s_rtick{tag}")
                self.s_hist, self.s_slot = sem(f"s_hist{tag}"), sem(f"s_slot{tag}")
                self.steps = Chain(None, self.s_slot)

            def count_block(self, dve, h):
                dve.wait_ge(self.s_hist, h + 1)
                nc.vector.tensor_scalar(mask[:, 0:self.n], self.block_of, lane_row[:, bass.ds(h, 1)], 0.0,
                                        ALU.is_equal, ALU.add, accum_out=hist[:, bass.ds(h, 1)]
                                        ).then_inc(self.s_hist, 1)

            def slots_of_block(self, h):
                self.steps.turn(h, 3)
                n = self.n
                return (
                    lambda dve: self.steps.on(dve)(nc.vector.tensor_scalar(
                        mask[:, 0:n], self.block_of, lane_row[:, bass.ds(h, 1)], None, ALU.is_equal)),
                    lambda dve: self.steps.on(dve)(nc.vector.tensor_tensor_scan(
                        count[:, 0:n], mask[:, 0:n], mask[:, 0:n], first[:, bass.ds(h, 1)], ALU.add, ALU.max)),
                    lambda dve: (dve.sem_inc(self.s_rtick), self.steps.on(dve)(nc.vector.copy_predicated(
                        slot[:, 0:n], mask[:, 0:n].bitcast(mybir.dt.int16), count[:, 0:n]))),
                )

            def place_blocks(self, counted):
                s_ps, s_tab = sem(f"s_ps{self.tag}"), sem(f"s_tab{self.tag}")
                own = ExitStack()
                itmp = sbuf(own, f"itmp{self.tag}", [P, HB], i32)
                tile_no = sbuf(own, f"tile_no{self.tag}", [P, NTB // P])
                over = sbuf(own, f"over{self.tag}", [P, NTB // P, BLOCKS])
                tb = sbuf(own, f"tb{self.tag}", [P, NTB // P])
                tbi = sbuf(own, f"tbi{self.tag}", [P, NTB // P], i32)
                both = view(banks(own, f"both{self.tag}")[:, 0, :], 2, HB)
                with nc.Block() as block:
                    @block.gpsimd
                    def _(pool):
                        nc.gpsimd.iota(tile_no[:, :], [[1, NTB // P]], base=0, channel_multiplier=NTB // P,
                                       allow_small_or_imprecise_dtypes=True).then_inc(s_tab, 1)

                    @block.tensor
                    def _(pe):
                        pe.wait_ge(self.s_hist, counted)
                        nc.tensor.matmul(both[:, 0, :], ones[:, :], hist[:, :], start=True, stop=True)
                        nc.tensor.matmul(both[:, 1, :], before[:, :], hist[:, :], start=True, stop=True
                                         ).then_inc(s_ps, 1)

                    @block.vector
                    def _(dve):
                        chain = vec_chain.on(dve)
                        dve.wait_ge(s_ps, 1)
                        nc.vector.tensor_copy(total[:, :], both[:, 0, :])
                        chain(nc.vector.tensor_scalar(tiles[:, :], both[:, 0, :], float(P - 1), None, ALU.add))
                        chain(nc.vector.tensor_copy(itmp[:, :], tiles[:, :]))
                        chain(nc.vector.tensor_scalar(itmp[:, :], itmp[:, :], 7, None, ALU.logical_shift_right))
                        chain(nc.vector.tensor_copy(tiles[:, :], itmp[:, :]))
                        chain(nc.vector.tensor_tensor_scan(ends[:, :], tiles[:, :], zeros[:, 0:HB], 0.0,
                                                           ALU.add, ALU.add))
                        chain(nc.vector.tensor_tensor(first[:, :], ends[:, :], tiles[:, :], ALU.subtract))
                        chain(nc.vector.tensor_scalar(first[:, :], first[:, :], float(P), -1.0, ALU.mult, ALU.add))
                        chain(nc.vector.tensor_tensor(first[:, :], first[:, :], both[:, 1, :], ALU.add))
                        dve.wait_ge(s_tab, 1)
                        chain(nc.vector.tensor_tensor(
                            over[:, :, :], ends[:, 0:BLOCKS].unsqueeze(1).to_broadcast([P, NTB // P, BLOCKS]),
                            tile_no[:, :].unsqueeze(2).to_broadcast([P, NTB // P, BLOCKS]), ALU.is_le))
                        chain(nc.vector.tensor_reduce(tb[:, :], over[:, :, :], AX, ALU.add))
                        chain(nc.vector.tensor_scalar(tb[:, :], tb[:, :], float(BLOCKS - 1), None, ALU.min))
                        nc.vector.tensor_copy(tbi[:, :], tb[:, :]).then_inc(s_tab, 1)

                    @block.sync
                    def _(sp):
                        sp.wait_ge(s_tab, 2)
                        sp.dma_start(self.table_dram.rearrange("(p t) -> p t", p=P), tbi[:, :]).then_inc(s_tab, 16)
                        sp.wait_ge(s_tab, 18)
                        sp.dma_start(self.table[0:1, :], self.table_dram.rearrange("(o t) -> o t", o=1)
                                     ).then_inc(s_tab, 16)
                        sp.wait_ge(s_tab, 34)
                own.close()

            def addresses(self, chain):
                n = self.n
                address = self.address
                chain(nc.vector.tensor_copy(address, slot[:, 0:n]))
                chain(nc.vector.tensor_scalar(address, address, P - 1, None, ALU.bitwise_and))
                chain(nc.vector.tensor_copy(count[:, 0:n], address))
                chain(nc.vector.tensor_copy(address, slot[:, 0:n]))
                chain(nc.vector.tensor_scalar(address, address, 7, None, ALU.logical_shift_right))
                chain(nc.vector.tensor_copy(slot[:, 0:n], address))
                chain(nc.vector.scalar_tensor_tensor(count[:, 0:n], count[:, 0:n], float(self.pitch), slot[:, 0:n],
                                                     ALU.mult, ALU.add))
                chain(nc.vector.tensor_copy(address, count[:, 0:n]))

        edge = src_node[:, 0:NT0]
        dst_block = src_block[:, 0:NT0]
        s_edge, s_first, s_next, s_viol, s_some = (sem(n) for n in ("s_edge", "s_first", "s_next", "s_viol", "s_some"))
        s_given, s_mfill = sem("s_given"), sem("s_mfill")
        own = ExitStack()
        next_ps = banks(own, "next_ps")
        some_ps = banks(own, "some_ps")
        first_block = sbuf(own, "first_block", [P, 1])
        viol = sbuf(own, "viol", [P, 2])
        limit = sbuf(own, "limit", [P, 1])
        by_dst = Rank("d", dst_block, NT0, address[:, 0:NT0], NTL, tile_block, tile_block_dram[0])
        with nc.Block() as block:
            @block.vector
            def _(dve):
                chain = vec_chain.on(dve)
                chain(nc.vector.tensor_scalar(edge, dst_raw[:, :], 7, None, ALU.logical_shift_right))
                chain(nc.vector.tensor_copy(dst_block, edge))
                nc.vector.tensor_copy(first_block[:, :], dst_block[:, 0:1]).then_inc(s_first, 1)
                chain(nc.vector.tensor_scalar(dst_raw[:, :], dst_raw[:, :], P - 1, None, ALU.bitwise_and))
                chain(nc.vector.scalar_tensor_tensor(edge, src_raw[:, :], float(P), dst_raw[:, :], ALU.mult, ALU.add))
                dve.sem_inc(s_edge)
                chain(nc.vector.tensor_tensor(mask[:, 0:NT0 - 1], dst_block[:, 0:NT0 - 1], dst_block[:, 1:NT0],
                                              ALU.is_gt))
                nc.vector.tensor_reduce(viol[:, 0:1], mask[:, 0:NT0 - 1], AX, ALU.max)
                chain(nc.vector.tensor_scalar(limit[:, :], part[:, :], float(P - 1), float(2 * P),
                                              ALU.is_equal, ALU.mult))
                dve.wait_ge(s_next, 1)
                chain(nc.vector.tensor_tensor(limit[:, :], limit[:, :], next_ps[:, 0, 0:1], ALU.add))
                chain(nc.vector.tensor_tensor(viol[:, 1:2], dst_block[:, NT0 - 1:NT0], limit[:, :], ALU.is_gt))
                dve.sem_inc(s_viol)
                dve.wait_ge(s_some, 1)
                chain(nc.vector.tensor_reduce(limit[:, :], some_ps[:, 0, 0:2], AX, ALU.add))
                chain(nc.vector.tensor_scalar(order_flag[:, :], limit[:, :], 0.0, None, ALU.is_equal))
                dve.sem_inc(by_dst.s_hist)
                with dve.Fori(0, BLOCKS) as h:
                    by_dst.count_block(dve, h)

            @block.tensor
            def _(pe):
                pe.wait_ge(s_first, 1)
                nc.tensor.matmul(next_ps[:, 0, 0:1], shift[:, :], first_block[:, :], start=True, stop=True
                                 ).then_inc(s_next, 1)
                pe.wait_ge(s_viol, 1)
                nc.tensor.matmul(some_ps[:, 0, 0:2], ones[:, :], viol[:, :], start=True, stop=True
                                 ).then_inc(s_some, 1)

            @block.sync
            def _(sp):
                sp.wait_ge(s_edge, 1)
                sp.dma_start(given_list[0:NT0, :].rearrange("r l -> (r l)").rearrange("(p t) -> p t", p=P), edge
                             ).then_inc(s_given, 16)
                m = messages.rearrange("(p t) w -> p (t w)", p=P)
                n = -(-NT2 * MROW // BANK)
                for j in range(n):
                    to = m[:, j * BANK:min((j + 1) * BANK, NT2 * MROW)]
                    sp.dma_start(to, zeros[:, 0:to.shape[1]]).then_inc(s_mfill, 16)
                sp.wait_ge(s_given, 16)
                sp.wait_ge(s_mfill, 16 * n)
        own.close()
        raw.close()
        by_dst.place_blocks(BLOCKS + 1)

        order = ExitStack()
        row_pairs = sbuf(order, "row_pairs", [P, ROWS, 2 * P], i32)
        work_i = row_pairs[:, :, :].rearrange("p g l -> p (g l)")
        tile_col = sbuf(order, "tile_col", [P, ROWS])
        at_edge = sbuf(order, "at_edge", [P, ROWS])
        filled = sbuf(order, "filled", [P, ROWS])
        row0 = sbuf(order, "row0", [P, ROWS], i32)
        row1 = sbuf(order, "row1", [P, ROWS], i32)
        offset = sbuf(order, "offset", [P, ROWS], i32)
        bit_i = sbuf(order, "bit_i", [P, ROWS], i32)
        bit = sbuf(order, "bit", [P, ROWS])
        jump = sbuf(order, "jump", [P, 2, BLOCKS])
        pay_i = sbuf(order, "pay_i", [P, 2, CH], i32)
        pay_v = sbuf(order, "pay_v", [P, 2, CH], i32)
        flat_ps = banks(order, "flat_ps", -(-ROWS * P // BANK))[:, :, :].rearrange("p a l -> p (a l)")
        line = acc_flat[:, 0:ROWS * 2 * P].rearrange("p (g l) -> p g l", l=2 * P)
        RUN = ROWS * 2 * P
        by_slot = acc_flat[:, RUN:RUN + NTL]
        s_pay, s_put, s_adr0 = sem("s_pay"), [sem(f"s_put{b}") for b in range(2)], sem("s_adr0")
        s_ptick, s_perm, s_back = sem("s_ptick"), sem("s_perm"), sem("s_back")
        s_col, s_rows, s_got, s_line, s_turned, s_f = (
            sem(n) for n in ("s_col", "s_rows", "s_got", "s_line", "s_turned", "s_f"))

        def in_order(dve):
            chain = Chain(dve, s_f)
            wide = [P, ROWS, BLOCKS - 1]
            over = acc_flat[:, 0:ROWS * (BLOCKS - 1)].rearrange("p (g b) -> p g b", g=ROWS)
            part_sum = acc_flat[:, RUN:RUN + ROWS * (BLOCKS - 1)].rearrange("p (g b) -> p g b", g=ROWS)
            chain(nc.vector.scalar_tensor_tensor(jump[:, 0, :], tiles[:, 0:BLOCKS], -float(P), total[:, 0:BLOCKS],
                                                 ALU.mult, ALU.add))
            chain(nc.vector.tensor_tensor(jump[:, 1, 0:BLOCKS - 1], total[:, 1:BLOCKS], jump[:, 0, 0:BLOCKS - 1],
                                          ALU.subtract))
            dve.wait_ge(s_col, 1)
            chain(nc.vector.tensor_tensor(over, ends[:, 0:BLOCKS - 1].unsqueeze(1).to_broadcast(wide),
                                          tile_col[:, :].unsqueeze(2).to_broadcast(wide), ALU.is_le))
            for to, n in ((at_edge, 0), (filled, 1)):
                chain(nc.vector.tensor_tensor(part_sum, over, jump[:, n, 0:BLOCKS - 1].unsqueeze(1).to_broadcast(wide),
                                              ALU.mult))
                chain(nc.vector.tensor_reduce(to[:, :], part_sum, AX, ALU.add))
            chain(nc.vector.scalar_tensor_tensor(at_edge[:, :], tile_col[:, :], float(P), at_edge[:, :],
                                                 ALU.mult, ALU.add))
            chain(nc.vector.scalar_tensor_tensor(filled[:, :], tile_col[:, :], -float(P), filled[:, :],
                                                 ALU.mult, ALU.add))
            chain(nc.vector.tensor_scalar(filled[:, :], filled[:, :], total[:, 0:1], None, ALU.add))
            chain(nc.vector.tensor_scalar(at_edge[:, :], at_edge[:, :], float(P * NT0), 0.0, ALU.min, ALU.max))
            chain(nc.vector.tensor_copy(offset[:, :], at_edge[:, :]))
            chain(nc.vector.tensor_scalar(row0[:, :], offset[:, :], 7, None, ALU.logical_shift_right))
            chain(nc.vector.tensor_scalar(row1[:, :], row0[:, :], 1, None, ALU.add))
            dve.sem_inc(s_rows)
            chain(nc.vector.tensor_scalar(offset[:, :], offset[:, :], P - 1, None, ALU.bitwise_and))
            dve.wait_ge(s_got, 16 * 2 * ROWS)
            chain(nc.vector.tensor_copy(line, row_pairs[:, :, :]))
            for k in reversed(range(7)):
                n, step = P - 1 + 2 ** k, 2 ** k
                moved = acc_flat[:, RUN:RUN + ROWS * n].rearrange("p (g l) -> p g l", g=ROWS)
                chain(nc.vector.tensor_scalar(bit_i[:, :], offset[:, :], k, 1, ALU.logical_shift_right,
                                              ALU.bitwise_and))
                chain(nc.vector.tensor_copy(bit[:, :], bit_i[:, :]))
                chain(nc.vector.tensor_tensor(moved, line[:, :, step:step + n], line[:, :, 0:n], ALU.subtract))
                chain(nc.vector.tensor_tensor(moved, moved, bit[:, :].unsqueeze(2).to_broadcast([P, ROWS, n]),
                                              ALU.mult))
                chain(nc.vector.tensor_tensor(line[:, :, 0:n], line[:, :, 0:n], moved, ALU.add))
            inside = acc_flat[:, RUN:RUN + ROWS * P].rearrange("p (g l) -> p g l", g=ROWS)
            chain(nc.vector.tensor_tensor(inside, lane_row[:, :].unsqueeze(1).to_broadcast([P, ROWS, P]),
                                          filled[:, :].unsqueeze(2).to_broadcast([P, ROWS, P]), ALU.is_lt))
            chain(nc.vector.tensor_scalar(line[:, :, 0:P], line[:, :, 0:P], 1.0, None, ALU.add))
            chain(nc.vector.tensor_tensor(line[:, :, 0:P], line[:, :, 0:P], inside, ALU.mult))
            chain(nc.vector.tensor_scalar(line[:, :, 0:P], line[:, :, 0:P], -1.0, None, ALU.add))
            dve.sem_inc(s_line)
            dve.wait_ge(s_turned, 1)
            chain(nc.vector.tensor_copy(by_slot, flat_ps[:, 0:NTL]))

        def by_rank(dve):
            with dve.Fori(0, BLOCKS) as h:
                for step in by_dst.slots_of_block(h):
                    step(dve)
            chain = Chain(dve, s_f)
            by_dst.addresses(chain)
            dve.sem_inc(s_adr0)
            dve.wait_ge(s_back, 16)
            chain(nc.vector.tensor_copy(by_slot, work_i[:, 0:NTL]))

        def flag_of(eng):
            return eng.value_load(order_flag[0:1, 0:1], min_val=0, max_val=1)

        with nc.Block() as block:
            @block.vector
            def _(dve):
                flag = flag_of(dve)
                with dve.If(flag == 1):
                    in_order(dve)
                with dve.Else():
                    by_rank(dve)

            @block.tensor
            def _(pe):
                flag = flag_of(pe)
                with pe.If(flag == 1):
                    pe.wait_ge(s_line, 1)
                    for g in range(ROWS):
                        last = nc.tensor.transpose(flat_ps[:, g * P:(g + 1) * P], line[:, g, 0:P], ident[:, :])
                    last.then_inc(s_turned, 1)
                with pe.Else():
                    pe.sem_inc(s_ptick)

            @block.scalar
            def _(act):
                def payload(at, b):
                    nc.scalar.copy(pay_i[:, b, :], address[:, bass.ds(at + b * CH, CH)])
                    nc.scalar.copy(pay_v[:, b, :], src_node[:, bass.ds(at + b * CH, CH)]).then_inc(s_pay, 1)
                flag = flag_of(act)
                with act.If(flag == 1):
                    act.sem_inc(s_ptick)
                with act.Else():
                    act.wait_ge(s_adr0, 1)
                    for b in range(2):
                        payload(0, b)
                    with act.Fori(1, NT0 // PAIR) as i:
                        for b in range(2):
                            act.wait_ge(s_put[b], i * (16 * CH))
                            act.sem_inc(s_ptick)
                            payload(i * PAIR, b)

            @block.gpsimd
            def _(pool):
                nc.gpsimd.iota(tile_col[:, :], [[P, ROWS]], base=0, channel_multiplier=1,
                               allow_small_or_imprecise_dtypes=True).then_inc(s_col, 1)
                flag = flag_of(pool)
                with pool.If(flag == 1):
                    pool.wait_ge(s_rows, 1)
                    for g in range(ROWS):
                        for half, row in ((0, row0), (1, row1)):
                            pool.indirect_dma_start(
                                out=row_pairs[:, g, half * P:(half + 1) * P], out_offset=None, in_=given_list,
                                in_offset=bass.IndirectOffsetOnAxis(ap=row[:, g:g + 1], axis=0)).then_inc(s_got, 16)
                with pool.Else():
                    with pool.Fori(0, NT0 // PAIR) as i:
                        for b in range(2):
                            pool.wait_ge(s_pay, i * 2 + (b + 1))
                            pool.sem_inc(s_ptick)
                            for k in range(CH):
                                pool.indirect_dma_start(
                                    out=slot_list,
                                    out_offset=bass.IndirectOffsetOnAxis(ap=pay_i[:, b, k:k + 1], axis=0),
                                    in_=pay_v[:, b, k:k + 1], in_offset=None).then_inc(s_put[b], 16)
                    for b in range(2):
                        pool.wait_ge(s_put[b], (NT0 // PAIR) * 16 * CH)
                    pool.sem_inc(s_perm)

            @block.sync
            def _(sp):
                flag = flag_of(sp)
                with sp.If(flag == 1):
                    sp.sem_inc(s_ptick)
                with sp.Else():
                    sp.wait_ge(s_perm, 1)
                    sp.dma_start(work_i[:, 0:NTL], slot_list.rearrange("(p t) w -> p (t w)", p=P)).then_inc(s_back, 16)

        with nc.Block() as block:
            @block.vector
            def _(dve):
                chain = vec_chain.on(dve)
                whole_i, some_i = work_i[:, 0:NTL], work_i[:, NTL:2 * NTL]
                empty = acc_flat[:, 0:NTL]
                nc.vector.tensor_scalar(empty, by_slot, 0.0, None, ALU.is_lt)
                chain(nc.vector.tensor_scalar(whole_i, by_slot, 0.0, None, ALU.max))
                chain(nc.vector.tensor_scalar(some_i, whole_i, P - 1, None, ALU.bitwise_and))
                chain(nc.vector.scalar_tensor_tensor(dst_lane[:, :], empty, float(NO_LANE), some_i,
                                                     ALU.mult, ALU.add))
                chain(nc.vector.tensor_scalar(whole_i, whole_i, 7, None, ALU.logical_shift_right))
                chain(nc.vector.scalar_tensor_tensor(src_node[:, :], empty, float(PAD_NODE), whole_i,
                                                     ALU.mult, ALU.add))
                nc.vector.tensor_scalar(some_i, src_node[:, :], P - 1, None, ALU.bitwise_and)
                chain(nc.vector.tensor_scalar(whole_i, src_node[:, :], 7, None, ALU.logical_shift_right))
                nc.vector.tensor_copy(src_lane[:, :], some_i)
                chain(nc.vector.tensor_copy(src_block[:, :], whole_i))
        order.close()
        by_src = Rank("s", src_block[:, 0:NT1], NT1, address[:, :], NT2, tile_block2, tile_block_dram[1])

        def one_hot(to, lanes, n, width=P):
            return nc.vector.tensor_tensor(to, lane_row[:, 0:width].unsqueeze(1).to_broadcast([P, n, width]),
                                           lanes.unsqueeze(2).to_broadcast([P, n, width]), ALU.is_equal)

        def blocks_of(table, tiles_from, engine, n=CH):
            return nc.values_load_multi_w_load_instructions(
                table[0:1, bass.ds(tiles_from, n)], engines=[engine], min_val=0, max_val=BLOCKS - 1,
                skip_runtime_bounds_check_because="the table of tiles' blocks is clamped to the last block")[1]

        def aggregate(tag, table, with_degrees):
            s_idx, s_row = sem(f"s_idx{tag}"), [sem(f"s_row{tag}{b}") for b in range(2)]
            s_hot, s_mm, s_tick = sem(f"s_hot{tag}"), sem(f"s_mm{tag}"), sem(f"s_tick{tag}")
            own = ExitStack()
            idx = sbuf(own, f"idx{tag}", [P, 2, CH], i32)
            rows = sbuf(own, f"rows{tag}", [P, 2, CH, F])
            hot = sbuf(own, f"hot{tag}", [P, 2, CH, P])
            sum_banks = banks(own, f"sum_banks{tag}", 4)
            sum_ps = sum_banks[:, :, :].rearrange("p a (b f) -> p (a b) f", f=F)
            if with_degrees:
                hot_dl = sbuf(own, f"hot_dl{tag}", [P, 2, CH, P], bf16)
                hot_sl = sbuf(own, f"hot_sl{tag}", [P, 2, CH, P], bf16)
                hot_sb = sbuf(own, f"hot_sb{tag}", [P, 2, CH, P], bf16)
                deg_ps = banks(own, f"deg_ps{tag}", 2)
            turns = NT1 // PAIR
            with nc.Block() as block:
                @block.scalar
                def _(act):
                    for b in range(2):
                        nc.scalar.copy(idx[:, b, :], src_node[:, b * CH:(b + 1) * CH]).then_inc(s_idx, 1)
                    with act.Fori(0, turns) as i:
                        for b in range(2):
                            act.wait_ge(s_row[b], i * (16 * CH) + 16 * CH)
                            act.sem_inc(s_tick)
                            nc.scalar.copy(idx[:, b, :], src_node[:, bass.ds(i * PAIR + (PAIR + b * CH), CH)]
                                           ).then_inc(s_idx, 1)

                @block.gpsimd
                def _(pool):
                    def gather(b):
                        for k in range(CH):
                            pool.indirect_dma_start(
                                out=rows[:, b, k, :], out_offset=None, in_=table,
                                in_offset=bass.IndirectOffsetOnAxis(ap=idx[:, b, k:k + 1], axis=0)
                            ).then_inc(s_row[b], 16)
                    for b in range(2):
                        pool.wait_ge(s_idx, b + 1)
                        gather(b)
                    with pool.Fori(0, turns) as i:
                        for b in range(2):
                            pool.wait_ge(s_idx, i * 2 + (b + 3))
                            pool.wait_ge(s_mm, i * 2 + (b + 3))
                            pool.sem_inc(s_tick)
                            gather(b)
                    for b in range(2):
                        pool.wait_ge(s_row[b], (turns + 1) * 16 * CH)

                @block.vector
                def _(dve):
                    if with_degrees:
                        dve.sem_inc(by_src.s_hist)
                    with dve.Fori(0, NT1 // QUAD) as i:
                        ranking = () if with_degrees else by_src.slots_of_block(i)
                        for q in range(4):
                            b = q % 2
                            at = bass.ds(i * QUAD + q * CH, CH)
                            dve.wait_ge(s_mm, i * 4 + (q + 1))
                            last = one_hot(hot[:, b, :, :], dst_lane[:, at], CH)
                            if with_degrees:
                                one_hot(hot_dl[:, b, :, :], dst_lane[:, at], CH)
                                one_hot(hot_sl[:, b, :, :], src_lane[:, at], CH)
                                last = one_hot(hot_sb[:, b, :, :], src_block[:, at], CH)
                            last.then_inc(s_hot, 1)
                            if with_degrees and q == 0:
                                by_src.count_block(dve, i)
                            if q < len(ranking):
                                ranking[q](dve)
                    chain = vec_chain.on(dve)
                    dve.wait_ge(s_mm, 2 * turns + 2)
                    chain(nc.vector.tensor_copy(sums, sum_ps[:, 0:BLOCKS, :]))
                    if with_degrees:
                        chain(nc.vector.tensor_copy(deg_dst[:, :], deg_ps[:, 0, 0:BLOCKS]))
                        chain(nc.vector.tensor_tensor(deg_sum[:, :], deg_dst[:, :], deg_ps[:, 1, 0:BLOCKS], ALU.add))
                    else:
                        by_src.addresses(chain)

                @block.tensor
                def _(pe):
                    pe.sem_inc(s_mm, 2)
                    for n in range(4):
                        nc.tensor.matmul(sum_banks[:, n, :], zeros[:, 0:P], zeros[:, 0:BANK], start=True, stop=True)
                    if with_degrees:
                        for n in range(2):
                            nc.tensor.matmul(deg_ps[:, n, 0:P], zeros[:, 0:P], zeros[:, 0:P], start=True, stop=True)
                    with pe.Fori(0, turns) as i:
                        for b in range(2):
                            at = blocks_of(tile_block, i * PAIR + b * CH, mybir.EngineType.PE)
                            pe.wait_ge(s_row[b], i * (16 * CH) + 16 * CH)
                            pe.wait_ge(s_hot, i * 2 + (b + 1))
                            pe.sem_inc(s_tick)
                            if with_degrees:
                                for k in range(CH):
                                    nc.tensor.matmul(deg_ps[:, 1, 0:P], hot_sl[:, b, k, :], hot_sb[:, b, k, :],
                                                     start=False, stop=True, skip_group_check=True)
                                for k in range(CH):
                                    nc.tensor.matmul(deg_ps[:, 0, bass.ds(at[k], 1)], hot_dl[:, b, k, :], ones_b[:, :],
                                                     start=False, stop=True, skip_group_check=True)
                            for k in range(CH):
                                to = sum_ps[:, bass.ds(at[k], 1), :].rearrange("p a f -> p (a f)")
                                last = nc.tensor.matmul(to, hot[:, b, k, :], rows[:, b, k, :], start=False, stop=True,
                                                        skip_group_check=True)
                            last.then_inc(s_mm, 1)

            own.close()

        aggregate("a", x_table, True)
        by_src.place_blocks(HB + 1)

        s_cat, s_nt, s_ht = sem("s_cat"), sem("s_nt"), sem("s_ht")
        s_node = [sem(f"s_node{j}") for j in range(TRACKS)]
        s_node_go = [sem(f"s_node_go{j}") for j in range(TRACKS)]
        own = ExitStack()
        cat = sbuf(own, "cat", [P, NBP, 2 * F])
        stage = sbuf(own, "stage", [P, TRACKS, P])
        stage_t = sbuf(own, "stage_t", [P, TRACKS, P])
        hidden = sbuf(own, "hidden", [HID1, TRACKS, GROUP * P])
        stage_ps = banks(own, "stage_ps", TRACKS)[:, :, 0:P]
        hidden_ps = banks(own, "hidden_ps", TRACKS)[0:HID1, :, :]
        out_banks = banks(own, "out_banks", TRACKS)
        STEPS = 7
        turns_n = GROUPS // TRACKS
        with nc.Block() as block:
            @block.vector
            def _(dve):
                chain = vec_chain.on(dve)
                nc.vector.tensor_scalar(r_deg[:, :], deg_dst[:, :], 1.0, None, ALU.max)
                chain(nc.vector.memset(cat[:, BLOCKS:, 0:F], 0.0))
                nc.vector.tensor_copy(cat[:, :, F:2 * F], x_nodes[:, :, :])
                chain(nc.vector.reciprocal(r_deg[:, :], r_deg[:, :]))
                chain(nc.vector.tensor_tensor(cat[:, 0:BLOCKS, 0:F], sums,
                                              r_deg[:, :].unsqueeze(2).to_broadcast([P, BLOCKS, F]), ALU.mult))
                dve.sem_inc(s_cat)
                with dve.Fori(0, turns_n) as g:
                    for j in range(TRACKS):
                        dve.wait_ge(s_node[j], g * STEPS + 6)
                        dve.sem_inc(s_nt)
                        nc.vector.tensor_copy(h_nodes[:, bass.ds(g * (TRACKS * GROUP) + j * GROUP, GROUP), :],
                                              view(out_banks[:, j, :], GROUP, 2 * F)).then_inc(s_node[j], 1)
                for j in range(TRACKS):
                    dve.wait_ge(s_node[j], turns_n * STEPS)

            @block.scalar
            def _(act):
                act.wait_ge(s_cat, 1)
                with act.Fori(0, turns_n) as g:
                    for j in range(TRACKS):
                        act.wait_ge(s_node_go[j], g + 1)
                        act.sem_inc(s_nt)
                        nc.scalar.copy(stage[:, j, :], cat[:, bass.ds(g * (TRACKS * GROUP) + j * GROUP, GROUP), :]
                                       .rearrange("p b f -> p (b f)")).then_inc(s_node[j], 1)
                    for j in range(TRACKS):
                        act.wait_ge(s_node[j], g * STEPS + 2)
                        act.sem_inc(s_nt)
                        nc.scalar.copy(stage_t[:, j, :], stage_ps[:, j, :]).then_inc(s_node[j], 1)
                    for j in range(TRACKS):
                        act.wait_ge(s_node[j], g * STEPS + 4)
                        act.sem_inc(s_nt)
                        nc.scalar.activation(hidden[:, j, :], hidden_ps[:, j, :], ACT.Relu, bias=b1c[:, 0:1]
                                             ).then_inc(s_node[j], 1)

            @block.tensor
            def _(pe):
                for j in range(TRACKS):
                    pe.sem_inc(s_node_go[j])
                with pe.Fori(0, turns_n) as g:
                    for j in range(TRACKS):
                        pe.wait_ge(s_node[j], g * STEPS + 1)
                        pe.sem_inc(s_nt)
                        nc.tensor.transpose(stage_ps[:, j, :], stage[:, j, :], ident[:, :]).then_inc(s_node[j], 1)
                    for j in range(TRACKS):
                        pe.wait_ge(s_node[j], g * STEPS + 3)
                        pe.sem_inc(s_nt)
                        for k in range(GROUP):
                            last = nc.tensor.matmul(hidden_ps[:, j, k * P:(k + 1) * P], w1[:, k, :], stage_t[:, j, :],
                                                    start=True, stop=True)
                        last.then_inc(s_node[j], 1)
                    for j in range(TRACKS):
                        pe.wait_ge(s_node[j], g * STEPS + 5)
                        pe.sem_inc(s_nt)
                        for k in range(GROUP):
                            last = nc.tensor.matmul(view(out_banks[:, j, :], GROUP, 2 * F)[:, k, :],
                                                    hidden[:, j, k * P:(k + 1) * P], w2[:, :], start=True, stop=True)
                        last.then_inc(s_node[j], 1)
                    for j in range(TRACKS):
                        pe.wait_ge(s_node[j], g * STEPS + 7)
                        pe.sem_inc(s_node_go[j])

            @block.sync
            def _(sp):
                for j in range(TRACKS):
                    sp.wait_ge(s_node[j], turns_n * STEPS)
                sp.dma_start(h_table.rearrange("(b l) f -> l b f", l=P), h_nodes[:, 0:BLOCKS, 0:F]).then_inc(s_ht, 16)
                sp.wait_ge(s_ht, 16)
        own.close()

        aggregate("b", h_table, False)

        own = ExitStack()
        t_sum = sbuf(own, "t_sum", [P, BLOCKS, F])
        t_sq = sbuf(own, "t_sq", [P, BLOCKS, F])
        t_mean = sbuf(own, "t_mean", [P, BLOCKS])
        t_var = sbuf(own, "t_var", [P, BLOCKS])
        t_deg = sbuf(own, "t_deg", [P, BLOCKS])
        rest = sbuf(own, "rest", [P, BLOCKS, ROW])
        s_sq, s_rt = sem("s_sq"), sem("s_rt")

        def wide(v):
            return v[:, :].unsqueeze(2).to_broadcast([P, BLOCKS, F])

        def layer_norm(dve, chain, to, turn):
            chain(nc.vector.tensor_reduce(t_mean[:, :], t_sum[:, :, :], AX, ALU.add))
            chain(nc.vector.tensor_scalar(t_mean[:, :], t_mean[:, :], 1.0 / F, None, ALU.mult))
            chain(nc.vector.tensor_tensor(t_sum[:, :, :], t_sum[:, :, :], wide(t_mean), ALU.subtract))
            chain(nc.vector.tensor_tensor(t_sq[:, :, :], t_sum[:, :, :], t_sum[:, :, :], ALU.mult))
            chain(nc.vector.tensor_reduce(t_var[:, :], t_sq[:, :, :], AX, ALU.add))
            chain(nc.vector.tensor_scalar(t_var[:, :], t_var[:, :], 1.0 / F, LN_EPS, ALU.mult, ALU.add))
            dve.sem_inc(s_sq)
            dve.wait_ge(s_rt, turn)
            chain(nc.vector.reciprocal(t_var[:, :], t_var[:, :]))
            chain(nc.vector.tensor_tensor(to, t_sum[:, :, :], wide(t_var), ALU.mult))

        s_y = sem("s_y")
        with nc.Block() as block:
            @block.vector
            def _(dve):
                chain = vec_chain.on(dve)
                chain(nc.vector.tensor_scalar(t_deg[:, :], deg_sum[:, :], 1e-5, None, ALU.max))
                chain(nc.vector.tensor_tensor(t_sum[:, :, :], sums, wide(r_deg), ALU.mult))
                chain(nc.vector.tensor_tensor(t_sum[:, :, :], t_sum[:, :, :], h_nodes[:, 0:BLOCKS, F:2 * F], ALU.add))
                chain(nc.vector.tensor_tensor(t_sum[:, :, :], t_sum[:, :, :],
                                              b2r[:, :].unsqueeze(1).to_broadcast([P, BLOCKS, F]), ALU.add))
                chain(nc.vector.tensor_tensor(t_sum[:, :, :], t_sum[:, :, :], x_nodes[:, 0:BLOCKS, :], ALU.add))
                layer_norm(dve, chain, y_nodes[:, 0:BLOCKS, 0:F], 2)
                chain(nc.vector.reciprocal(y_nodes[:, 0:BLOCKS, F], t_deg[:, :]))
                chain(nc.vector.tensor_copy(y_parts[:, :, 0, :], y_nodes[:, 0:BLOCKS, :]))
                chain(nc.vector.tensor_tensor(rest[:, :, :], y_nodes[:, 0:BLOCKS, :], y_parts[:, :, 0, :], ALU.subtract))
                chain(nc.vector.tensor_copy(y_parts[:, :, 1, :], rest[:, :, :]))
                chain(nc.vector.tensor_tensor(y_parts[:, :, 2, :], rest[:, :, :], y_parts[:, :, 1, :], ALU.subtract))
                dve.sem_inc(s_y)

            @block.scalar
            def _(act):
                act.wait_ge(s_sq, 1)
                nc.scalar.sqrt(t_deg[:, :], t_deg[:, :]).then_inc(s_rt, 1)
                nc.scalar.sqrt(t_var[:, :], t_var[:, :]).then_inc(s_rt, 1)

            @block.sync
            def _(sp):
                sp.wait_ge(s_y, 1)
                sp.dma_start(y_table.rearrange("(b l) f -> l b f", l=P), y_nodes[:, 0:BLOCKS, :]).then_inc(s_y, 16)
                sp.wait_ge(s_y, 17)
        own.close()

        s_idx, s_adr, s_msg = sem("s_idx3"), sem("s_adr3"), sem("s_msg3")
        s_row = [sem(f"s_row3{q}") for q in range(4)]
        s_put = [sem(f"s_put3{b}") for b in range(2)]
        s_hot, s_hott, s_hotc, s_ownr = sem("s_hot3"), sem("s_hott"), sem("s_hotc"), sem("s_own3")
        s_xc, s_xt, s_xtc, s_hid, s_hidr, s_map = (sem(n) for n in ("s_xc", "s_xt", "s_xtc", "s_hid", "s_hidr", "s_map"))
        s_free = sem("s_free")
        s_msg2 = sem("s_msg2")
        s_mapu, s_mm, s_add, s_tick, s_d = (sem(n) for n in ("s_mapu", "s_mm3", "s_add3", "s_tick3", "s_d3"))
        own = ExitStack()
        idx = sbuf(own, "idx3", [P, 4, CH], i32)
        adr = sbuf(own, "adr3", [P, 2, CH], i32)
        rows = sbuf(own, "rows3", [P, 4, CH, ROW])
        hot = sbuf(own, "hot3", [P, 2, CH, P], bf16)
        hot_t = sbuf(own, "hot_t", [P, CH, P], bf16)
        xx = sbuf(own, "xx", [P, 2, CH, 2, F])
        inv = sbuf(own, "inv", [P, 2, CH, 2])
        xx_t = sbuf(own, "xx_t", [P, 2, P])
        hid = sbuf(own, "hid", [P, CH, P])
        v = sbuf(own, "v", [P, CH, 2, F])
        t = sbuf(own, "t", [P, CH, 2, F])
        t2 = sbuf(own, "t2", [P, CH, 2, F])
        w = sbuf(own, "w", [P, CH, 2, F])
        n2 = sbuf(own, "n2", [P, CH, 2])
        d = sbuf(own, "d", [P, CH, 2])
        msg = sbuf(own, "msg", [P, 2, CH, 2, MROW])
        msg_b = msg[:, :, :, :, :].rearrange("p b k e m -> p (b k e m)").bitcast(bf16).rearrange(
            "p (b k e m) -> p b k e m", b=2, k=CH, e=2)
        hot_ps = banks(own, "hot_ps")[:, 0, :].bitcast(bf16).rearrange("p (k l) -> p k l", l=P)
        own_ps = view(banks(own, "own_ps")[:, 0, :], CH, ROW)
        xx_ps = view(banks(own, "xx_ps")[:, 0, :], 2, P)
        hid_ps = banks(own, "hid_ps", 2)[:, :, :].rearrange("p a (k l) -> p (a k) l", l=P)
        map_ps = view(banks(own, "map_ps")[:, 0, :], CH, 2 * F)
        sum_ps = view(banks(own, "sum_ps3")[:, 0, :], CH, F)
        turns = NT1 // QUAD
        DSTEPS = 18
        with nc.Block() as block:
            @block.gpsimd
            def _(pool):
                def gather(q):
                    for k in range(CH):
                        pool.indirect_dma_start(
                            out=rows[:, q, k, :], out_offset=None, in_=y_table,
                            in_offset=bass.IndirectOffsetOnAxis(ap=idx[:, q, k:k + 1], axis=0)
                        ).then_inc(s_row[q], 16)
                pool.sem_inc(s_free, 2)
                for q in range(3):
                    pool.wait_ge(s_idx, q + 1)
                    gather(q)
                with pool.Fori(0, turns) as i:
                    for q in range(4):
                        b, c = q % 2, i * 4 + q
                        pool.wait_ge(s_idx, c + 4)
                        if q == 0:
                            pool.wait_ge(s_xc, c + 1)
                        else:
                            pool.wait_ge(s_xc, c)
                        pool.wait_ge(s_msg, c + 1)
                        pool.wait_ge(s_adr, c + 1)
                        pool.sem_inc(s_tick)
                        for k in range(CH):
                            pool.indirect_dma_start(
                                out=messages, out_offset=bass.IndirectOffsetOnAxis(ap=adr[:, b, k:k + 1], axis=0),
                                in_=msg[:, b, k, 0, :], in_offset=None).then_inc(s_put[b], 16)
                        gather((q + 3) % 4)
                        pool.wait_ge(s_put[b], i * (2 * 16 * CH) + 16 * CH * (q // 2 + 1))
                        pool.sem_inc(s_free)
                for q in range(4):
                    pool.wait_ge(s_row[q], (turns + (q < 3)) * 16 * CH)

            @block.scalar
            def _(act):
                def copy_hot(c):
                    act.wait_ge(s_hott, c + 1)
                    act.sem_inc(s_tick)
                    nc.scalar.copy(hot_t[:, :, :], hot_ps).then_inc(s_hotc, 1)
                for q in range(3):
                    nc.scalar.copy(idx[:, q, :], src_node[:, q * CH:(q + 1) * CH]).then_inc(s_idx, 1)

                def ends(c, q, row_count, idx_from, used):
                    b = q % 2
                    copy_hot(c)
                    act.wait_ge(s_row[q], row_count)
                    act.wait_ge(s_ownr, c + 1)
                    if used is not None:
                        act.wait_ge(s_msg2, used)
                    act.sem_inc(s_tick)
                    nc.scalar.copy(xx[:, b, :, 0, :], rows[:, q, :, 0:F])
                    nc.scalar.copy(xx[:, b, :, 1, :], own_ps[:, :, 0:F])
                    nc.scalar.copy(inv[:, b, :, 1], rows[:, q, :, F])
                    nc.scalar.copy(inv[:, b, :, 0], own_ps[:, :, F]).then_inc(s_xc, 1)
                    nc.scalar.copy(idx[:, (q + 3) % 4, :], src_node[:, bass.ds(idx_from, CH)]).then_inc(s_idx, 1)
                    act.wait_ge(s_xt, c + 1)
                    act.sem_inc(s_tick)
                    nc.scalar.copy(xx_t[:, :, :], xx_ps[:, :, :]).then_inc(s_xtc, 1)
                    act.wait_ge(s_hid, c + 1)
                    act.sem_inc(s_tick)
                    for half in range(2):
                        last = nc.scalar.activation(hid[:, half * 4:half * 4 + 4, :],
                                                    hid_ps[:, half * 4:half * 4 + 4, :], ACT.Relu,
                                                    bias=v1c[:, 0:1])
                    last.then_inc(s_hidr, 1)
                ends(0, 0, 16 * CH, 3 * CH, None)
                with act.Fori(0, turns) as i:
                    for q in range(4):
                        b, c = q % 2, i * 4 + q
                        act.wait_ge(s_free, c + 1)
                        act.sem_inc(s_tick)
                        nc.scalar.copy(msg_b[:, b, :, 0, PARTS * F], src_lane[:, bass.ds(i * QUAD + q * CH, CH)])
                        nc.scalar.copy(adr[:, b, :], address[:, bass.ds(i * QUAD + q * CH, CH)]).then_inc(s_adr, 1)
                        ends(c + 1, (q + 1) % 4, i * (16 * CH) + 16 * CH * ((q + 1) // 4 + 1),
                             i * QUAD + (q + 4) * CH, c + 1)

            @block.tensor
            def _(pe):
                def own_rows(c, b, at):
                    blocks = blocks_of(tile_block, at, mybir.EngineType.PE)
                    pe.wait_ge(s_hot, c + 1)
                    pe.sem_inc(s_tick)
                    for k in range(CH):
                        last = nc.tensor.transpose(hot_ps[:, k, :], hot[:, b, k, :], ident_b[:, :])
                    last.then_inc(s_hott, 1)
                    pe.wait_ge(s_hotc, c + 1)
                    pe.sem_inc(s_tick)
                    for k in range(CH):
                        for j in range(PARTS):
                            last = nc.tensor.matmul(
                                own_ps[:, k, :], hot_t[:, k, :],
                                y_parts[:, bass.ds(blocks[k], 1), j, :].rearrange("p a f -> p (a f)"),
                                start=(j == 0), stop=(j == PARTS - 1))
                    last.then_inc(s_ownr, 1)
                def hiddens(c, b):
                    pe.wait_ge(s_xc, c + 1)
                    pe.sem_inc(s_tick)
                    for g in range(2):
                        last = nc.tensor.transpose(
                            xx_ps[:, g, :], xx[:, b, 4 * g:4 * g + 4, :, :].rearrange("p k e f -> p (k e f)"),
                            ident[:, :])
                    last.then_inc(s_xt, 1)
                    pe.wait_ge(s_xtc, c + 1)
                    pe.sem_inc(s_tick)
                    for k in range(CH):
                        last = nc.tensor.matmul(hid_ps[:, k, :], v1[:, k % GROUP, :], xx_t[:, k // GROUP, :],
                                                start=True, stop=True)
                    last.then_inc(s_hid, 1)

                def maps(c):
                    pe.wait_ge(s_hidr, c + 1)
                    pe.wait_ge(s_mapu, c + 1)
                    pe.sem_inc(s_tick)
                    for k in range(CH):
                        last = nc.tensor.matmul(map_ps[:, k, :], hid[:, k, :], v2[:, :], start=True, stop=True)
                    last.then_inc(s_map, 1)
                own_rows(0, 0, 0)
                hiddens(0, 0)
                maps(0)
                with pe.Fori(0, turns) as i:
                    for q in range(4):
                        b, c = q % 2, i * 4 + q
                        own_rows(c + 1, 1 - b, i * QUAD + (q + 1) * CH)
                        hiddens(c + 1, 1 - b)
                        pe.wait_ge(s_msg2, c + 2)
                        pe.wait_ge(s_add, c + 1)
                        pe.sem_inc(s_tick)
                        for k in range(CH):
                            for j in range(PARTS):
                                last = nc.tensor.matmul(sum_ps[:, k, :], hot[:, b, k, :],
                                                        msg_b[:, b, k, 1, j * F:(j + 1) * F],
                                                        start=(j == 0), stop=(j == PARTS - 1))
                        last.then_inc(s_mm, 1)
                        maps(c + 1)

            @block.vector
            def _(dve):
                def pairs(x):
                    return x.unsqueeze(3).to_broadcast([P, CH, 2, F])

                dve.sem_inc(s_mapu)
                dve.sem_inc(s_msg2)
                nc.vector.memset(msg[:, :, :, :, :], 0.0)
                nc.vector.memset(acc[:, :, :, :], 0.0).then_inc(s_add, 1)
                for b in range(2):
                    one_hot(hot[:, b, :, :], dst_lane[:, b * CH:(b + 1) * CH], CH).then_inc(s_hot, 1)
                steps = Chain(dve, s_d)
                with dve.Fori(0, turns) as i:
                    steps.turn(i, 4 * DSTEPS)
                    for q in range(4):
                        b, c = q % 2, i * 4 + q
                        x_both = xx[:, b, :, :, :]
                        dve.wait_ge(s_map, c + 1)
                        steps(nc.vector.tensor_tensor(
                            v[:, :, :, :].rearrange("p k e f -> p k (e f)"), map_ps[:, :, :],
                            v2r[:, :].unsqueeze(1).to_broadcast([P, CH, 2 * F]), ALU.add))
                        dve.sem_inc(s_mapu)
                        nc.vector.tensor_tensor(t[:, :, :, :], v[:, :, :, :], v[:, :, :, :], ALU.mult)
                        steps(nc.vector.tensor_tensor(t2[:, :, :, :], v[:, :, :, :], x_both, ALU.mult))
                        nc.vector.tensor_reduce(d[:, :, :], t2[:, :, :, :], AX, ALU.add)
                        steps(nc.vector.tensor_reduce(n2[:, :, :], t[:, :, :, :], AX, ALU.add))
                        steps(nc.vector.tensor_scalar(n2[:, :, :], n2[:, :, :], NORM_EPS2, 0.5, ALU.max, ALU.mult))
                        steps(nc.vector.reciprocal(n2[:, :, :], n2[:, :, :]))
                        steps(nc.vector.tensor_tensor(d[:, :, :], d[:, :, :], n2[:, :, :], ALU.mult))
                        steps(nc.vector.tensor_tensor(t[:, :, :, :], v[:, :, :, :], pairs(d[:, :, :]), ALU.mult))
                        nc.vector.tensor_tensor(w[:, :, 0, :], x_both[:, :, 1, :], t[:, :, 1, :], ALU.subtract)
                        steps(nc.vector.tensor_tensor(w[:, :, 1, :], x_both[:, :, 0, :], t[:, :, 0, :], ALU.subtract))
                        steps(nc.vector.tensor_tensor(t2[:, :, :, :], v[:, :, :, :], w[:, :, :, :], ALU.mult))
                        steps(nc.vector.tensor_reduce(d[:, :, :], t2[:, :, :, :], AX, ALU.add))
                        steps(nc.vector.tensor_tensor(d[:, :, :], d[:, :, :], n2[:, :, :], ALU.mult))
                        steps(nc.vector.tensor_tensor(t[:, :, :, :], v[:, :, :, :], pairs(d[:, :, :]), ALU.mult))
                        steps(nc.vector.tensor_tensor(w[:, :, :, :], w[:, :, :, :], t[:, :, :, :], ALU.subtract))
                        steps(nc.vector.tensor_tensor(t[:, :, :, :], w[:, :, :, :], pairs(inv[:, b, :, :]), ALU.mult))
                        to = [msg_b[:, b, :, :, j * F:(j + 1) * F] for j in range(PARTS)]
                        dve.wait_ge(s_free, c + 1)
                        steps(nc.vector.tensor_copy(to[0], t[:, :, :, :]))
                        steps(nc.vector.tensor_tensor(t2[:, :, :, :], t[:, :, :, :], to[0], ALU.subtract))
                        steps(nc.vector.tensor_copy(to[1], t2[:, :, :, :]))
                        steps(nc.vector.tensor_tensor(to[2], t2[:, :, :, :], to[1], ALU.subtract))
                        dve.sem_inc(s_msg)
                        dve.sem_inc(s_msg2)
                        at = blocks_of(tile_block, i * QUAD + q * CH, mybir.EngineType.DVE)
                        dve.wait_ge(s_mm, c + 1)
                        dve.wait_ge(s_add, c + 1)
                        for k in range(CH):
                            to = acc[:, k, bass.ds(at[k], 1), 0:F].rearrange("p a f -> p (a f)")
                            last = nc.vector.tensor_tensor(to, to, sum_ps[:, k, :], ALU.add)
                        last.then_inc(s_add, 1)
                        one_hot(hot[:, b, :, :], dst_lane[:, bass.ds(i * QUAD + (q + 2) * CH, CH)], CH
                                ).then_inc(s_hot, 1)
                chain = vec_chain.on(dve)
                dve.wait_ge(s_add, 4 * turns + 1)
                for half in (4, 2, 1):
                    chain(nc.vector.tensor_tensor(acc[:, 0:half, :, 0:F], acc[:, 0:half, :, 0:F],
                                                  acc[:, half:2 * half, :, 0:F], ALU.add))
        own.close()

        own = ExitStack()
        DEEP = 4
        s_in = [sem(f"s_in{q}") for q in range(DEEP)]
        s_hot, s_mm, s_tick = sem("s_hot4"), sem("s_mm4"), sem("s_tick4")
        got = sbuf(own, "got", [P, DEEP, CH, MROW])
        got_b = got[:, :, :, :].rearrange("p q k m -> p (q k m)").bitcast(bf16).rearrange(
            "p (q k m) -> p q k m", q=DEEP, k=CH)
        hot = sbuf(own, "hot4", [P, DEEP, CH, P], bf16)
        sum_banks = banks(own, "sum_banks4", 4)
        sum_ps = sum_banks[:, :, :].rearrange("p a (b f) -> p (a b) f", f=F)
        m_rows = messages.rearrange("(p t) w -> p t w", p=P)
        turns4 = NT2 // (DEEP * CH)
        with nc.Block() as block:
            @block.sync
            def _(sp):
                with sp.Fori(0, turns4) as i:
                    for q in range(DEEP):
                        sp.wait_ge(s_mm, i * DEEP + (q + 1))
                        sp.sem_inc(s_tick)
                        sp.dma_start(got[:, q, :, :], m_rows[:, bass.ds(i * (DEEP * CH) + q * CH, CH), :]
                                     ).then_inc(s_in[q], 16)

            @block.vector
            def _(dve):
                with dve.Fori(0, turns4) as i:
                    for q in range(DEEP):
                        dve.wait_ge(s_in[q], i * 16 + 16)
                        dve.sem_inc(s_tick)
                        one_hot(hot[:, q, :, :], got_b[:, q, :, PARTS * F], CH).then_inc(s_hot, 1)
                chain = vec_chain.on(dve)
                dve.wait_ge(s_mm, NT2 // CH + DEEP)
                chain(nc.vector.tensor_tensor(acc[:, 0, :, 0:F], acc[:, 0, :, 0:F], sum_ps[:, 0:BLOCKS, :], ALU.add))

            @block.tensor
            def _(pe):
                pe.sem_inc(s_mm, DEEP)
                for n in range(4):
                    nc.tensor.matmul(sum_banks[:, n, :], zeros[:, 0:P], zeros[:, 0:BANK], start=True, stop=True)
                with pe.Fori(0, turns4) as i:
                    turn_at = blocks_of(tile_block2, i * (DEEP * CH), mybir.EngineType.PE, DEEP * CH)
                    for q in range(DEEP):
                        at = turn_at[q * CH:(q + 1) * CH]
                        pe.wait_ge(s_in[q], i * 16 + 16)
                        pe.wait_ge(s_hot, i * DEEP + (q + 1))
                        pe.sem_inc(s_tick)
                        for k in range(CH):
                            to = sum_ps[:, bass.ds(at[k], 1), :].rearrange("p a f -> p (a f)")
                            for j in range(PARTS):
                                last = nc.tensor.matmul(to, hot[:, q, k, :], got_b[:, q, k, j * F:(j + 1) * F],
                                                        start=False, stop=True, skip_group_check=True)
                        last.then_inc(s_mm, 1)
        own.close()

        own = ExitStack()
        t_sum = sbuf(own, "t_sum5", [P, BLOCKS, F])
        t_sq = sbuf(own, "t_sq5", [P, BLOCKS, F])
        t_mean = sbuf(own, "t_mean5", [P, BLOCKS])
        t_var = sbuf(own, "t_var5", [P, BLOCKS])
        s_fin = sem("s_fin")
        y = y_nodes[:, 0:BLOCKS, 0:F]
        with nc.Block() as block:
            @block.vector
            def _(dve):
                chain = vec_chain.on(dve)
                chain(nc.vector.tensor_tensor(t_sum[:, :, :], acc[:, 0, :, 0:F],
                                              y_nodes[:, 0:BLOCKS, F:ROW].to_broadcast([P, BLOCKS, F]), ALU.mult))
                chain(nc.vector.tensor_tensor(t_sum[:, :, :], t_sum[:, :, :], y, ALU.add))
                chain(nc.vector.tensor_scalar(t_sum[:, :, :], t_sum[:, :, :], 0.0, None, ALU.max))
                chain(nc.vector.tensor_tensor(t_sum[:, :, :], t_sum[:, :, :], y, ALU.add))
                layer_norm(dve, chain, t_sq[:, :, :], 3)
                dve.sem_inc(s_fin)

            @block.scalar
            def _(act):
                act.wait_ge(s_sq, 2)
                nc.scalar.sqrt(t_var[:, :], t_var[:, :]).then_inc(s_rt, 1)

            @block.sync
            def _(sp):
                sp.wait_ge(s_fin, 1)
                whole = NODES // P
                sp.dma_start(out[0:whole * P, :].rearrange("(b l) f -> l b f", l=P), t_sq[:, 0:whole, :]
                             ).then_inc(s_fin, 16)
                sp.dma_start(out[whole * P:NODES, :], t_sq[0:NODES - whole * P, whole, :]).then_inc(s_fin, 16)
                sp.wait_ge(s_fin, 33)
        own.close()


_INS = ['x', 'src', 'dst', 'L0_gnn_W1_l', 'L0_gnn_b1', 'L0_gnn_W1_r', 'L0_gnn_W2_l', 'L0_gnn_b2', 'L0_gnn_W2_r',
        'L1_gnn_W1', 'L1_gnn_b1', 'L1_gnn_W2', 'L1_gnn_b2']
_OUTS = [((NODES, F), 'float32')]


def kernel(**inputs):
    import numpy as _np
    import concourse.bacc as _bacc
    from concourse import mybir as _mybir
    from concourse.bass_utils import run_bass_kernel_spmd as _run

    nc = _bacc.Bacc("TRN2", target_bir_lowering=False, num_devices=1)
    arrays, args = {}, []
    for name in _INS:
        a = _np.ascontiguousarray(inputs[name])
        arrays[f"in_{name}_dram"] = a
        args.append(nc.dram_tensor(f"in_{name}_dram", a.shape, _mybir.dt.from_np(a.dtype), kind="ExternalInput").ap())
    for i, (shape, dtype) in enumerate(_OUTS):
        dt = _mybir.dt.from_np(_np.dtype(dtype))
        args.append(nc.dram_tensor(f"out_{i}_dram", shape, dt, kind="ExternalOutput").ap())
    gnn(nc, *args)
    r = _run(nc, [arrays], core_ids=[0])
    got = tuple(r.results[0][f"out_{i}_dram"] for i in range(len(_OUTS)))
    return got[0]
```
